# Optimizing a Trainium2 kernel written in Bass

```python
import numpy as np
import jax
import jax.numpy as jnp

def _softmax(x, axis=-1):
    return jax.nn.softmax(x, axis=axis)

def _gelu(x):
    return jax.nn.gelu(x, approximate=True)

def _silu(x):
    return jax.nn.silu(x)

def _sigmoid(x):
    return jax.nn.sigmoid(x)

def _layernorm(x, axis=-1, eps=1e-05):
    m = jnp.mean(x, axis=axis, keepdims=True)
    v = jnp.var(x, axis=axis, keepdims=True)
    return (x - m) / jnp.sqrt(v + eps)

def _scatter_add(tgt, idx, src, axis=0):
    return tgt.at[idx].add(src)

def _segment_sum(src, seg, n):
    return jax.ops.segment_sum(src, seg, n)
kernel_name = 'mk_seq_postln_d2_jaxref_r8_b7a24e'

def setup_inputs(seed: int=0):
    np.random.seed(seed)
    _w = jnp.asarray

    def _L0_attn_setup():
        import jax, jax.numpy as jnp
        import numpy as np
        B, L, D_MODEL = (2, 256, 128)
        D_STATE, D_CONV, EXPAND = (8, 4, 2)
        D_INNER = EXPAND * D_MODEL
        DT_RANK = (D_MODEL + 15) // 16
        key = jax.random.key(seed)
        ks = jax.random.split(key, 8)
        s = 0.02
        x = jax.random.normal(ks[0], (B, L, D_MODEL), dtype=jnp.float32)
        W_in = jax.random.normal(ks[1], (D_MODEL, 2 * D_INNER), dtype=jnp.float32) * s
        dw_kernel = jax.random.normal(ks[2], (D_CONV, D_INNER), dtype=jnp.float32) * s
        pw_kernel = jax.random.normal(ks[3], (D_INNER, D_INNER), dtype=jnp.float32) * s
        conv_bias = jnp.zeros((D_INNER,), dtype=jnp.float32)
        W_x = jax.random.normal(ks[4], (D_INNER, DT_RANK + 2 * D_STATE), dtype=jnp.float32) * s
        W_dt = jax.random.normal(ks[5], (DT_RANK, D_INNER), dtype=jnp.float32) * s
        b_dt = jnp.zeros((D_INNER,), dtype=jnp.float32)
        A_init = np.repeat(np.arange(1, D_STATE + 1, dtype=np.float32), D_INNER).reshape(D_INNER, D_STATE)
        A_log = jnp.asarray(np.log(A_init))
        D = jnp.ones((D_INNER,), dtype=jnp.float32)
        W_out = jax.random.normal(ks[6], (D_INNER, D_MODEL), dtype=jnp.float32) * s
        return {'x': x, 'W_in': W_in, 'dw_kernel': dw_kernel, 'pw_kernel': pw_kernel, 'conv_bias': conv_bias, 'W_x': W_x, 'W_dt': W_dt, 'b_dt': b_dt, 'A_log': A_log, 'D': D, 'W_out': W_out}
    _L0_attn_in = _L0_attn_setup()

    def _L0_ffn_setup():
        import jax, jax.numpy as jnp
        import numpy as np
        key = jax.random.key(seed)
        kx, kw = jax.random.split(key)
        x = jax.random.normal(kx, (32, 512, 128), dtype=jnp.float32)
        weight = jax.random.normal(kw, (128, 128), dtype=jnp.float32) * 0.01
        return {'x': x, 'weight': weight}
    _L0_ffn_in = _L0_ffn_setup()

    def _L1_attn_setup():
        import jax, jax.numpy as jnp
        import numpy as np
        B, S, DM, H, DH = (2, 256, 128, 16, 64)
        HID = H * DH

        def _xavier(key, shape):
            fan_out, fan_in = shape
            lim = float(np.sqrt(6.0 / (fan_in + fan_out)))
            return jax.random.uniform(key, shape, jnp.float32, -lim, lim)

        def _gla_scan(q, k, v, g):
            qt = jnp.moveaxis(q, 1, 0)
            kt = jnp.moveaxis(k, 1, 0)
            vt = jnp.moveaxis(v, 1, 0)
            gt = jnp.moveaxis(g, 1, 0)

            def step(s, inp):
                qi, ki, vi, gi = inp
                s = jnp.exp(gi)[:, :, None, None] * s + ki[..., :, None] * vi[..., None, :]
                o = jnp.einsum('bhk,bhkv->bhv', qi, s)
                return (s, o)
            s0 = jnp.zeros(q.shape[0:1] + q.shape[2:] + q.shape[-1:], q.dtype)
            _, o = jax.lax.scan(step, s0, (qt, kt, vt, gt))
            return jnp.moveaxis(o, 0, 1)
        key = jax.random.key(seed)
        ks = jax.random.split(key, 8)
        return {'x': jax.random.normal(ks[0], (B, S, DM), jnp.float32), 'Wq': _xavier(ks[1], (HID, DM)), 'Wk': _xavier(ks[2], (HID, DM)), 'Wv': _xavier(ks[3], (HID, DM)), 'Wo': _xavier(ks[4], (DM, HID)), 'Wg': _xavier(ks[5], (HID, DM)), 'Wog': _xavier(ks[6], (HID, DM)), 'Wd': _xavier(ks[7], (H, DM)), 'bd': jnp.full((H,), -2.0, jnp.float32), 'norm_w': jnp.ones((HID,), jnp.float32)}
    _L1_attn_in = _L1_attn_setup()

    def _L1_ffn_setup():
        import jax, jax.numpy as jnp
        import numpy as np
        E = 8
        TOPK = 2
        D = 128
        F = 512
        B, S = (2, 64)

        def _gmm(x, W, expert_onehot):
            return jnp.einsum('te,td,edf->tf', expert_onehot, x, W)
        key = jax.random.key(seed)
        k1, k2, k3, k4, k5 = jax.random.split(key, 5)
        scale_d = 1.0 / np.sqrt(D)
        scale_f = 1.0 / np.sqrt(F)
        return {'inputs': jax.random.normal(k1, (B, S, D), jnp.float32), 'gate_kernel': jax.random.normal(k2, (D, E), jnp.float32) * scale_d, 'w0': jax.random.normal(k3, (E, D, F), jnp.float32) * scale_d, 'w1': jax.random.normal(k4, (E, D, F), jnp.float32) * scale_d, 'wo': jax.random.normal(k5, (E, F, D), jnp.float32) * scale_f}
    _L1_ffn_in = _L1_ffn_setup()
    _d = {'L0_attn_x': _L0_attn_in['x'], 'L0_attn_W_in': _L0_attn_in['W_in'], 'L0_attn_dw_kernel': _L0_attn_in['dw_kernel'], 'L0_attn_pw_kernel': _L0_attn_in['pw_kernel'], 'L0_attn_conv_bias': _L0_attn_in['conv_bias'], 'L0_attn_W_x': _L0_attn_in['W_x'], 'L0_attn_W_dt': _L0_attn_in['W_dt'], 'L0_attn_b_dt': _L0_attn_in['b_dt'], 'L0_attn_A_log': _L0_attn_in['A_log'], 'L0_attn_D': _L0_attn_in['D'], 'L0_attn_W_out': _L0_attn_in['W_out'], 'L0_ffn_weight': _L0_ffn_in['weight'], 'L1_attn_Wq': _L1_attn_in['Wq'], 'L1_attn_Wk': _L1_attn_in['Wk'], 'L1_attn_Wv': _L1_attn_in['Wv'], 'L1_attn_Wo': _L1_attn_in['Wo'], 'L1_attn_Wg': _L1_attn_in['Wg'], 'L1_attn_Wog': _L1_attn_in['Wog'], 'L1_attn_Wd': _L1_attn_in['Wd'], 'L1_attn_bd': _L1_attn_in['bd'], 'L1_attn_norm_w': _L1_attn_in['norm_w'], 'L1_ffn_gate_kernel': _L1_ffn_in['gate_kernel'], 'L1_ffn_w0': _L1_ffn_in['w0'], 'L1_ffn_w1': _L1_ffn_in['w1'], 'L1_ffn_wo': _L1_ffn_in['wo']}
    _x0 = _d['L0_attn_x']
    _d['L0_attn_x'] = jax.random.normal(jax.random.fold_in(jax.random.key(seed), 1), (16, 512, 128), dtype=_x0.dtype)
    del _x0
    return _d

def reference(L0_attn_x, L0_attn_W_in, L0_attn_dw_kernel, L0_attn_pw_kernel, L0_attn_conv_bias, L0_attn_W_x, L0_attn_W_dt, L0_attn_b_dt, L0_attn_A_log, L0_attn_D, L0_attn_W_out, L0_ffn_weight, L1_attn_Wq, L1_attn_Wk, L1_attn_Wv, L1_attn_Wo, L1_attn_Wg, L1_attn_Wog, L1_attn_Wd, L1_attn_bd, L1_attn_norm_w, L1_ffn_gate_kernel, L1_ffn_w0, L1_ffn_w1, L1_ffn_wo):

    def _L0_attn_ref(x, W_in, dw_kernel, pw_kernel, conv_bias, W_x, W_dt, b_dt, A_log, D, W_out):
        import jax, jax.numpy as jnp
        import numpy as np
        B, L, D_MODEL = (2, 256, 128)
        D_STATE, D_CONV, EXPAND = (8, 4, 2)
        D_INNER = EXPAND * D_MODEL
        DT_RANK = (D_MODEL + 15) // 16
        d_inner, d_state = A_log.shape
        dt_rank = W_dt.shape[0]
        d_conv = dw_kernel.shape[0]
        bsz = x.shape[0]
        xz = x @ W_in
        x_in, z = jnp.split(xz, 2, axis=-1)
        xp = jnp.pad(x_in, ((0, 0), (d_conv - 1, 0), (0, 0)))
        xc = jax.lax.conv_general_dilated(xp, dw_kernel[:, None, :], window_strides=(1,), padding='VALID', dimension_numbers=('NWC', 'WIO', 'NWC'), feature_group_count=d_inner)
        xc = jax.nn.silu(xc @ pw_kernel + conv_bias)
        x_dbl = xc @ W_x
        delta = x_dbl[..., :dt_rank]
        Bm = x_dbl[..., dt_rank:dt_rank + d_state]
        C = x_dbl[..., dt_rank + d_state:]
        delta = jax.nn.softplus(delta @ W_dt + b_dt)
        A = -jnp.exp(A_log)
        deltaA = jnp.exp(jnp.einsum('bld,dn->bldn', delta, A))
        deltaB_u = jnp.einsum('bld,bln,bld->bldn', delta, Bm, xc)

        def step(h, inp):
            dA_t, dBu_t, C_t = inp
            h = dA_t * h + dBu_t
            y_t = jnp.einsum('bn,bdn->bd', C_t, h)
            return (h, y_t)
        h0 = jnp.zeros((bsz, d_inner, d_state), dtype=x.dtype)
        elems = (deltaA.transpose(1, 0, 2, 3), deltaB_u.transpose(1, 0, 2, 3), C.transpose(1, 0, 2))
        _, ys = jax.lax.scan(step, h0, elems)
        y = ys.transpose(1, 0, 2)
        y = y + xc * D
        y = y * jax.nn.silu(z)
        return y @ W_out

    def _L0_ffn_ref(x, weight):
        import jax, jax.numpy as jnp
        import numpy as np
        b_weight = jnp.sign(weight)
        return jnp.einsum('bsi,oi->bso', x, b_weight)

    def _L1_attn_ref(x, Wq, Wk, Wv, Wo, Wg, Wog, Wd, bd, norm_w):
        import jax, jax.numpy as jnp
        import numpy as np
        B, S, DM, H, DH = (2, 256, 128, 16, 64)
        HID = H * DH

        def _xavier(key, shape):
            fan_out, fan_in = shape
            lim = float(np.sqrt(6.0 / (fan_in + fan_out)))
            return jax.random.uniform(key, shape, jnp.float32, -lim, lim)

        def _gla_scan(q, k, v, g):
            qt = jnp.moveaxis(q, 1, 0)
            kt = jnp.moveaxis(k, 1, 0)
            vt = jnp.moveaxis(v, 1, 0)
            gt = jnp.moveaxis(g, 1, 0)

            def step(s, inp):
                qi, ki, vi, gi = inp
                s = jnp.exp(gi)[:, :, None, None] * s + ki[..., :, None] * vi[..., None, :]
                o = jnp.einsum('bhk,bhkv->bhv', qi, s)
                return (s, o)
            s0 = jnp.zeros(q.shape[0:1] + q.shape[2:] + q.shape[-1:], q.dtype)
            _, o = jax.lax.scan(step, s0, (qt, kt, vt, gt))
            return jnp.moveaxis(o, 0, 1)
        b, s, _ = x.shape
        q = (x @ Wq.T).reshape(b, s, H, DH)
        k = (x @ Wk.T).reshape(b, s, H, DH)
        v = (x @ Wv.T).reshape(b, s, H, DH)
        log_decay = -jax.nn.softplus(x @ Wd.T + bd)
        gate = jax.nn.sigmoid((x @ Wg.T).reshape(b, s, H, DH))
        k_gated = k * gate
        out = _gla_scan(q, k_gated, v, log_decay)
        out = out.reshape(b, s, HID)
        eps = jnp.finfo(out.dtype).eps
        out = out * jax.lax.rsqrt(jnp.mean(out * out, -1, keepdims=True) + eps) * norm_w
        out = out * jax.nn.sigmoid(x @ Wog.T)
        return out @ Wo.T

    def _L1_ffn_ref(inputs, gate_kernel, w0, w1, wo):
        import jax, jax.numpy as jnp
        import numpy as np
        E = 8
        TOPK = 2
        D = 128
        F = 512
        B, S = (2, 64)

        def _gmm(x, W, expert_onehot):
            return jnp.einsum('te,td,edf->tf', expert_onehot, x, W)
        dtype = inputs.dtype
        gate_logits = jnp.einsum('bsd,de->bse', inputs, gate_kernel)
        weights, selected_experts = jax.lax.top_k(gate_logits, TOPK)
        weights = jax.nn.softmax(weights.astype(jnp.float32), axis=-1).astype(dtype)
        inputs_2d = jnp.reshape(inputs, (-1, D))
        flat_sel = jnp.ravel(selected_experts)
        sort_idx = jnp.argsort(flat_sel)
        rep = jnp.repeat(inputs_2d, TOPK, axis=0)
        sorted_hidden = jnp.take(rep, sort_idx, axis=0)
        T = flat_sel.shape[0]
        group_sizes = jnp.zeros((E,), jnp.int32).at[flat_sel].add(1)
        expert_ids = jnp.repeat(jnp.arange(E), group_sizes, total_repeat_length=T)
        onehot = jax.nn.one_hot(expert_ids, E, dtype=dtype)
        layer_1 = _gmm(sorted_hidden, w0, onehot)
        layer_2 = _gmm(sorted_hidden, w1, onehot)
        intermediate = jax.nn.silu(layer_1) * layer_2
        layer_3 = _gmm(intermediate, wo, onehot)
        unsort = jnp.take(layer_3, jnp.argsort(sort_idx), axis=0)
        combined = unsort * jnp.ravel(weights)[:, None]
        out = jnp.sum(combined.reshape(-1, TOPK, D), axis=1)
        return out.reshape(inputs.shape).astype(dtype)
    x = L0_attn_x
    x = _layernorm(x + _L0_attn_ref(x, L0_attn_W_in, L0_attn_dw_kernel, L0_attn_pw_kernel, L0_attn_conv_bias, L0_attn_W_x, L0_attn_W_dt, L0_attn_b_dt, L0_attn_A_log, L0_attn_D, L0_attn_W_out), axis=-1)
    x = _layernorm(x + _L0_ffn_ref(x, L0_ffn_weight), axis=-1)
    x = _layernorm(x + _L1_attn_ref(x, L1_attn_Wq, L1_attn_Wk, L1_attn_Wv, L1_attn_Wo, L1_attn_Wg, L1_attn_Wog, L1_attn_Wd, L1_attn_bd, L1_attn_norm_w), axis=-1)
    x = _layernorm(x + _L1_ffn_ref(x, L1_ffn_gate_kernel, L1_ffn_w0, L1_ffn_w1, L1_ffn_wo), axis=-1)
    return x

_drawn_inputs = setup_inputs


def setup_inputs(seed=0):
    import zlib

    import numpy as np

    out = dict(_drawn_inputs(seed))
    spreads = {'L0_attn_conv_bias': (0.0, 0.439),
     'L0_attn_b_dt': (0.0, 0.8),
     'L0_attn_D': (1.0, 0.6),
     'L1_attn_bd': (-2.0, 0.2),
     'L1_attn_norm_w': (1.0, 0.2)}
    factors = {'L0_attn_W_in': 3.702,
     'L0_attn_dw_kernel': 8.0,
     'L0_attn_pw_kernel': 8.0,
     'L0_attn_W_x': 8.0,
     'L0_attn_W_dt': 8.0,
     'L0_attn_A_log': 8.0,
     'L0_attn_W_out': 3.296}
    for name, (base, spread) in spreads.items():
        noise = np.random.default_rng([zlib.crc32(name.encode()), seed]).standard_normal(out[name].shape)
        drawn = base * np.exp(spread * noise) if base else spread * noise
        out[name] = jnp.asarray(drawn.astype(out[name].dtype))
    for name, factor in factors.items():
        out[name] = (out[name] * factor).astype(out[name].dtype)
    return out
```

```python
from contextlib import ExitStack

import numpy as np

import concourse.bass as bass
from concourse import mybir

P = 128
T = 512
TILES = T // P
HALVES = 2
STATES = 8
TAPS = 4
HEADS = 16
DH = 64
PAIRS = HEADS // 2
HID = HEADS * DH
EXPERTS = 8
FF = 512
FCHUNKS = FF // P
PART2, PART3, DT_ROW, ROWS = 64, 96, 32, 112

F32 = mybir.dt.float32
BF16 = mybir.dt.bfloat16
I32 = mybir.dt.int32
ALU = mybir.AluOpType
ACT = mybir.ActivationFunctionType
AX = mybir.AxisListType
LN_EPS = 1e-5
LN_STEPS = 11
RMS_EPS = float(np.finfo(np.float32).eps)


def head_of(g, h):
    return 8 * (g // 2) + g % 2 + 2 * h


def of_group(g):
    return slice(head_of(g, 0), head_of(g, 3) + 1, 2)


def shape_constants():
    part_rows = (0, PART2, PART3)
    sel = np.zeros((ROWS, HEADS, P), np.float32)
    selpair = np.zeros((ROWS, PAIRS, P), np.float32)
    for r in part_rows:
        for h in range(HEADS):
            sel[r + h, h, :] = 1.0
            selpair[r + h, h // 2, (h % 2) * DH:(h % 2 + 1) * DH] = 1.0
    j, i = np.mgrid[0:P, 0:P]
    future = np.where(i < j, -1e30, 0.0).astype(np.float32)
    eye = np.eye(P, dtype=np.float32)
    from_last = eye - (j == P - 1)
    earlier = (j < i).astype(np.float32)
    return {
        "sel": sel, "nsel": -sel, "nselpair": -selpair, "future": np.tile(future, (1, 4)),
        "rev": np.tile(EXPERTS - np.arange(EXPERTS, dtype=np.float32), (P, 1)),
        "eye": eye, "from_last": from_last.astype(np.float32), "earlier": earlier,
    }


def at(it, per_round, k):
    return it * per_round + k


def after(eng, sem, value):
    if isinstance(value, int) and value <= 0:
        return
    eng.wait_ge(sem, value)


def first(it):
    return isinstance(it, int) and it == 0


def moe_tiles(tokens):
    worst = 2 * tokens // P + EXPERTS
    return -(-worst // MOE_BODY) * MOE_BODY


class Ring:

    def __init__(self, banks, filled, drained, uses):
        self.banks, self.filled, self.drained = banks, filled, drained
        self.n = len(filled)
        self.place = {}
        self.per = [0] * self.n
        for k, use in enumerate(uses):
            b = k % self.n
            self.per[b] += 1
            self.place[use] = (b, self.per[b])

    def bank(self, use):
        return self.banks[:, self.place[use][0], :]

    def free_sem(self, use):
        return self.drained[self.place[use][0]]

    def full_sem(self, use):
        return self.filled[self.place[use][0]]

    def free_at(self, use, it):
        b, k = self.place[use]
        return at(it, self.per[b], k - 1)

    def full_at(self, use, it):
        b, k = self.place[use]
        return at(it, self.per[b], k)



L0_USES = (["xT", "u0", "u1", "z0", "z1", "xdbl", "dt0", "dt1"]
           + [f"{c}{n}" for n in range(STATES) for c in "BC"] + ["mix", "x1T", "ffn"])


def l1_uses():
    uses = ["x2T", "wd"]
    for u in range(PAIRS):
        uses += [f"q{u}", f"g{u}", f"k{u}"]
        uses += ["cpT"] if u == 3 else ["cpd"] if u == 5 else []
    for c in range(TILES):
        uses += [f"v0_{c}", f"v1_{c}", f"o0_{c}", f"o1_{c}", f"e0_{c}", f"e1_{c}", f"kT0_{c}", f"kT1_{c}",
                 f"D0_{c}", f"S0_{c}"]
        uses += [f"OT0_{c - 1}", f"OT1_{c - 1}"] if c else []
        uses += [f"D1_{c}", f"S1_{c}"]
        uses += [f"wo_{c - 1}"] if c else []
        uses += [f"D2_{c}", f"S2_{c}", f"D3_{c}", f"S3_{c}"]
        uses += [f"U_{c}"] if c < TILES - 1 else []
    last = TILES - 1
    return uses + [f"OT0_{last}", f"OT1_{last}", f"wo_{last}", "x3T", "route"]


MOE_BODY = 8
ZERO_ROWS = 8
MOE_LOAD = 4
UNITS = 16

def build(nc, a, out):
    B = a["x"].shape[0]
    TOK_TILES = B * TILES
    ROW_TILES = moe_tiles(B * T)
    with ExitStack() as ctx:
        attention = ExitStack()

        def sb(name, shape, dt=F32):
            return attention.enter_context(nc.sbuf_tensor(name, shape, dt))

        def sb_kept(name, shape, dt=F32):
            return ctx.enter_context(nc.sbuf_tensor(name, shape, dt))

        logits = sb_kept("logits", [P, TOK_TILES, EXPERTS])
        eye = sb_kept("eye", [P, P])
        minus_half = sb_kept("minus_half", [P, TILES])
        rms_eps = sb_kept("rms_eps", [P, 1])
        earlier = sb_kept("earlier", [P, P], BF16)
        ones_bf = sb_kept("ones_bf", [P, P], BF16)
        rev = sb_kept("rev", [P, EXPERTS])
        tile_no = sb_kept("tile_no", [1, ROW_TILES])
        stats = sb_kept("stats", [P, TILES, 6])
        mean = sb_kept("mean", [P, TILES])
        apart = sb_kept("apart", [P, TILES])
        var = sb_kept("var", [P, TILES])
        rstd = sb_kept("rstd", [P, TILES])

        def sem(name):
            return ctx.enter_context(nc.semaphore(name))

        eye_bf = sb("eye_bf", [P, P], BF16)
        sel = sb("sel", [ROWS, HEADS, P], BF16)
        nsel = sb("nsel", [ROWS, HEADS, P], BF16)
        nselpair = sb("nselpair", [ROWS, PAIRS, P], BF16)
        future = sb("future", [P, 4 * P], BF16)
        from_last = sb("from_last", [P, P])
        taps = sb("taps", [P, HALVES, TAPS])
        w_conv = sb("w_conv", [P, TAPS, 2 * P])
        w_z = sb("w_z", [P, 2 * P])
        w_x = sb("w_x", [P, HALVES, ROWS])
        w_dt = sb("w_dt", [P, 2 * P])
        b_conv = sb("b_conv", [P, HALVES])
        b_dt = sb("b_dt", [P, HALVES])
        d_skip = sb("d_skip", [P, HALVES])
        a_neg = sb("a_neg", [P, HALVES, STATES])
        a_log = sb("a_log", [P, HALVES, STATES])
        w_out = sb("w_out", [P, HALVES, P])
        w_ffn = sb("w_ffn", [P, P])
        w_sign = sb("w_sign", [P, P])
        w_less = sb("w_less", [P, P])
        w_q = sb("w_q", [P, HID])
        w_k = sb("w_k", [P, HID])
        w_v = sb("w_v", [P, HID])
        w_g = sb("w_g", [P, HID])
        w_og = sb("w_og", [P, HID])
        w_o = sb("w_o", [P, PAIRS, P])
        norm_w = sb("norm_w", [P, PAIRS])
        w_d = sb("w_d", [P, ROWS])
        b_d = sb("b_d", [ROWS, 1])
        w_route = sb("w_route", [P, EXPERTS])
        ones = sb("ones", [ROWS, P])

        x_tok = sb("x_tok", [P, TILES, P])
        xT = sb("xT", [P, TAPS - 1 + T])
        xc = sb("xc", [P, HALVES, T])
        th = sb("th", [P, HALVES, T])
        sz = sb("sz", [P, HALVES, T])
        parts = sb("parts", [ROWS, T], BF16)
        rest = sb("rest", [ROWS, T])
        dt_raw = sb("dt_raw", [P, T])
        delta = sb("delta", [P, HALVES, T])
        du = sb("du", [P, HALVES, T])
        decay = sb("decay", [P, 2, HALVES, T])
        push = sb("push", [P, HALVES, T])
        hs = sb("hs", [P, HALVES, T])
        ch = sb("ch", [P, 2, HALVES, T])
        y = sb("y", [P, HALVES, T])
        x1 = sb("x1", [P, TILES, P])
        x1T = sb("x1T", [P, T])
        x2_new = sb("x2_new", [P, TILES, P])

        x3 = sb("x3", [P, TILES, P])
        x2T = sb("x2T", [P, T])
        sp_in = sb("sp_in", [ROWS, T])
        sp_ln = sb("sp_ln", [ROWS, T])
        fall = sb("fall", [ROWS, T])
        fall_parts = sb("fall_parts", [ROWS, T], BF16)
        fall_rest = sb("fall_rest", [ROWS, T])
        fall_tok = sb("fall_tok", [P, TILES * HEADS])
        to_end = sb("to_end", [P, TILES, HEADS])
        q = sb("q", [P, PAIRS, T])
        k = sb("k", [P, PAIRS, T])
        tg = sb("tg", [P, 2, T])
        v = sb("v", [P, HID])
        tog = sb("tog", [P, HID])
        from_start = sb("from_start", [P, PAIRS, P])
        qd = sb("qd", [P, PAIRS, P])
        kd = sb("kd", [P, HEADS, DH])
        E = sb("E", [P, 2, 4 * P])
        pw = E[:, 0, :].rearrange("p (c n) -> p c n", c=HALVES)
        w_inT = E[:, 1, 0:2 * P].rearrange("p (c n) -> p c n", c=HALVES)
        w_tap = E[:, 1, 2 * P:4 * P].rearrange("p (c n) -> p c n", c=HALVES)
        S = sb("S", [P, 2, 4 * P])
        state = sb("state", [P, PAIRS, DH])
        o = sb("o", [P, HID])
        oT = sb("oT", [P, PAIRS, P])
        sq = sb("sq", [P, T], BF16)
        ssq = sb("ssq", [P, TILES, 2])
        rms = sb("rms", [P, TILES])
        x3T = sb("x3T", [P, T])
        zeros = q[:, 0:2, :].rearrange("p a n -> p (a n)")
        attention.close()

        w_0 = sb_kept("w_0", [P, EXPERTS * FF])
        w_1 = sb_kept("w_1", [P, EXPERTS * FF])
        w_2 = sb_kept("w_2", [P, EXPERTS * FF])
        tokens = sb_kept("tokens", [P, TOK_TILES, P])
        best = sb_kept("best", [P, 2, TOK_TILES])
        place = sb_kept("place", [P, 2, TOK_TILES])
        hot = sb_kept("hot", [P, 2, TOK_TILES, EXPERTS])
        hot_bf = sb_kept("hot_bf", [P, TOK_TILES, EXPERTS], BF16)
        work = sb_kept("work", [P, TOK_TILES, EXPERTS])
        rank = sb_kept("rank", [P, TOK_TILES, EXPERTS])
        total = sb_kept("total", [P, EXPERTS, TOK_TILES])
        upto = sb_kept("upto", [P, EXPERTS, TOK_TILES])
        ones_r = sb_kept("ones_r", [P, TOK_TILES])
        count_i = sb_kept("count_i", [P, EXPERTS], I32)
        tiles_of = sb_kept("tiles_of", [P, EXPERTS])
        ends = sb_kept("ends", [P, EXPERTS])
        base = sb_kept("base", [P, EXPERTS])
        share = sb_kept("share", [P, 2, TOK_TILES])
        row_of = sb_kept("row_of", [P, 2, TOK_TILES], I32)
        past = sb_kept("past", [1, ROW_TILES, EXPERTS])
        expert_f = sb_kept("expert_f", [1, ROW_TILES])
        expert_i = sb_kept("expert_i", [1, ROW_TILES], I32)
        rows_in = sb_kept("rows_in", [P, 2, MOE_LOAD, P])
        rowsT = sb_kept("rowsT", [P, 2, MOE_LOAD * P])
        tanh_h = sb_kept("tanh_h", [P, 2, FF])
        act_h = sb_kept("act_h", [P, 2, FF])
        hT = sb_kept("hT", [P, 2, FF])
        rows_out = sb_kept("rows_out", [P, 2, MOE_LOAD, P])
        gathered = sb_kept("gathered", [P, 2, TILES, 2, P])
        final = sb_kept("final", [P, 2, TILES, P])

        x3_dram = nc.dram_tensor("x3_scratch", [B, T, P], F32, kind="Internal").ap().rearrange(
            "b (c p) d -> b p c d", p=P)
        rows_dram = nc.dram_tensor("rows_scratch", [ROW_TILES * P, P], F32, kind="Internal").ap()
        results_dram = nc.dram_tensor("results_scratch", [ROW_TILES * P, P], F32, kind="Internal").ap()

        banks = ctx.enter_context(nc.psum_tensor("banks", [P, 8, T], F32))
        l0_banks, l1_banks, o_banks = banks[:, 0:3, :], banks[:, 3:6, :], banks[:, 6:8, :]
        bank_h = banks[:, 0:4, :].rearrange("p (u m) f -> p u m f", u=2)
        bank_hT, bank_y, bank_rows = banks[:, 4:6, :], banks[:, 6, :], banks[:, 7, :]

        s_weights = sem("weights_loaded")
        s_wtap = sem("w_tap_ready")
        s_wmul = sem("w_conv_multiplied")
        s_wconv = sem("w_conv_copied")
        s_prep = sem("weights_prepared")
        s_alog = sem("a_log_exp")
        s_sign = sem("sign_steps")
        l0 = Ring(l0_banks, [sem(f"l0_filled{b}") for b in range(3)],
                  [sem(f"l0_drained{b}") for b in range(3)], L0_USES)
        l1 = Ring(l1_banks, [sem(f"l1_filled{b}") for b in range(3)],
                  [sem(f"l1_drained{b}") for b in range(3)], l1_uses())
        s_x_loaded = sem("x_loaded")
        s_hu = sem("half_u_ready")
        s_tanh = sem("tanh_ready")
        s_xc = sem("xc_ready")
        s_dt_raw = sem("dt_raw_ready")
        s_split = sem("split_steps")
        s_dtb = sem("dt_biased")
        s_sp = sem("softplus_steps")
        s_delta = sem("delta_ready")
        s_du = sem("du_ready")
        s_decay = sem("decay_ready")
        s_push = sem("push_ready")
        s_scan = sem("scan_ready")
        s_ch = sem("ch_ready")
        s_ysum = sem("y_summed")
        s_ygate = sem("y_gate_steps")
        s_y = sem("y_ready")
        s_ln0 = sem("ln0_steps")
        s_ln1 = sem("ln1_steps")
        s_x1 = sem("x1_ready")
        s_x1T = sem("x1T_ready")
        s_x2 = sem("x2_ready")
        s_x2_taken = sem("x2_taken")

        s_x2T = sem("x2T_ready")
        s_dsp = sem("decay_softplus_act")
        s_dlog = sem("decay_softplus_ready")
        s_fall = sem("fall_ready")
        s_fsplit = sem("fall_split_steps")
        s_ftok = sem("fall_tok_ready")
        s_toend = sem("to_end_ready")
        s_q = sem("q_ready")
        s_tg = sem("gate_tanh_ready")
        s_k = sem("k_ready")
        s_v = sem("v_ready")
        s_tog = sem("out_gate_tanh_ready")
        s_fs = sem("from_start_ready")
        s_qd = sem("q_decayed")
        s_kd = sem("k_decayed")
        s_E = sem("mask_ready")
        s_S = sem("scores_ready")
        s_O = sem("o_filled")
        s_osq = sem("o_squared")
        s_og = sem("o_gated")
        s_decst = sem("state_decayed")
        s_state = sem("state_ready")
        s_oT = sem("oT_ready")
        s_rms = sem("rms_steps")
        s_rms_pow = sem("rms_ready")
        s_ln3 = sem("ln3_steps")
        s_rstd0 = sem("ln0_scale")
        s_rms_eps = sem("rms_eps_added")
        s_rstd1 = sem("ln1_scale")
        s_rstd3 = sem("ln3_scale")
        s_x3 = sem("x3_ready")
        s_x3T = sem("x3T_ready")
        s_x3_stored = sem("x3_stored")
        s_cleared = sem("rows_cleared")
        s_zero = sem("zeros_ready")
        s_w_moe = sem("expert_weights_loaded")
        s_tokens = sem("tokens_loaded")
        s_route = sem("route_steps")
        s_counted = sem("ranks_counted")
        s_share = sem("share_exp")
        s_rows_known = sem("row_of_ready")
        s_expert = sem("expert_ready")
        s_scattered = sem("rows_scattered")
        s_rows_in = [sem("rows_in_loaded0"), sem("rows_in_loaded1")]
        s_turned = sem("rows_turned")
        s_rowsT = sem("rowsT_ready")
        s_h = sem("h_multiplied")
        s_tanh_h = sem("tanh_h_ready")
        s_silu = sem("silu_ready")
        s_act_h = sem("act_h_ready")
        s_h_turned = sem("h_turned")
        s_hT = sem("hT_ready")
        s_y_tile = sem("result_multiplied")
        s_rows_out = sem("result_copied")
        s_results = [sem("results_stored0"), sem("results_stored1")]
        s_gathered = [sem("results_gathered0"), sem("results_gathered1")]
        s_mixed = sem("results_mixed")
        s_ln4 = sem("ln4_steps")
        s_rstd4 = sem("ln4_scale")
        s_final = sem("final_ready")
        s_out = [sem("out_stored0"), sem("out_stored1")]

        loads = [
            (eye[:], a["eye"]), (eye_bf[:], a["eye_bf"]), (sel[:], a["sel"]), (nsel[:], a["nsel"]),
            (nselpair[:], a["nselpair"]), (future[:], a["future"]), (from_last[:], a["from_last"]),
            (w_inT[:], a["w_inT"]), (taps[:], a["taps"]), (pw[:], a["pw"]), (w_z[:], a["w_z"]), (w_x[:], a["w_x"]),
            (w_dt[DT_ROW:DT_ROW + 8, :], a["w_dt"]), (b_conv[:], a["b_conv"]), (b_dt[:], a["b_dt"]),
            (d_skip[:], a["d_skip"]), (a_log[:], a["a_log"]), (w_out[:], a["w_out"]), (w_ffn[:], a["w_ffn"]),
            (w_q[:], a["w_q"]), (w_k[:], a["w_k"]), (w_v[:], a["w_v"]), (w_g[:], a["w_g"]), (w_og[:], a["w_og"]),
            (w_o[:], a["w_o"]), (norm_w[:], a["norm_w"]), (w_d[:], a["w_d"]), (b_d[:], a["b_d"]),
            (w_route[:], a["w_route"]), (earlier[:], a["earlier"]), (ones_bf[:], a["ones_bf"]), (rev[:], a["rev"]),
            (tile_no[:], a["tile_no"]),
        ]
        WEIGHTS = 16 * len(loads)
        PREPARED = 9 + PAIRS
        x_dram = a["x"].rearrange("b (c p) d -> b p c d", p=P)
        out_dram = out.rearrange("b (c p) d -> b p c d", p=P)
        zero_dram = rows_dram.rearrange("(n p r) d -> n p (r d)", p=P, r=ZERO_ROWS)
        rows_in_dram = rows_dram.rearrange("(n c p) d -> n p c d", c=MOE_LOAD, p=P)
        rows_out_dram = results_dram.rearrange("(n c p) d -> n p c d", c=MOE_LOAD, p=P)

        def drained(eng, ring, it, *uses):
            last = {}
            for use in uses:
                bank, count = ring.place[use]
                last[bank] = max(last.get(bank, 0), count)
            for bank, count in last.items():
                eng.wait_ge(ring.drained[bank], at(it, ring.per[bank], count))

        ROUTE_HOT = 12
        ROUTE_BEST = ROUTE_HOT + 1
        ROUTE_TAKEN = ROUTE_BEST + 3

        block = ctx.enter_context(nc.Block())

        def rounds(eng, body):
            body(0, None)
            body(1, 0)
            with eng.Fori(2, B) as r:
                body(r, r - 1)
            body(None, B - 1)

        def attention_over(eng):
            drained(eng, l1, B - 1, "route")
            eng.wait_ge(s_x3, B * TILES)

        @block.sync
        def _(sp):
            for dst, src in loads:
                sp.dma_start(dst, src).then_inc(s_weights, 16)

            def body(i, j):
                if i is not None:
                    if not first(i):
                        drained(sp, l0, i - 1, "mix")
                    sp.dma_start(x_tok[:], x_dram[bass.ds(i, 1)].rearrange("b p c d -> (b p) c d")
                                 ).then_inc(s_x_loaded, 16)
                if j is not None:
                    sp.wait_ge(s_x3, at(j, TILES, TILES))
                    sp.dma_start(x3_dram[bass.ds(j, 1)].rearrange("b p c d -> (b p) c d"), x3[:]
                                 ).then_inc(s_x3_stored, 16)

            sp.wait_ge(s_zero, 1)
            for n in range(ROW_TILES // ZERO_ROWS):
                sp.dma_start(zero_dram[n], zeros).then_inc(s_cleared, 16)
            rounds(sp, body)

            attention_over(sp)
            sp.wait_ge(s_x3_stored, 16 * B)
            for b in range(B):
                sp.dma_start(tokens[:, b * TILES:(b + 1) * TILES, :], x3_dram[b]).then_inc(s_tokens, 16)
            for dst, name in ((w_0, "w_0"), (w_1, "w_1"), (w_2, "w_2")):
                sp.dma_start(dst[:], a[name]).then_inc(s_w_moe, 16)
            sp.wait_ge(s_scattered, 16 * 2 * TOK_TILES)

            def load_rows(i):
                for n in range(2):
                    g = 2 * i + n
                    if not first(i):
                        sp.wait_ge(s_turned, g - 1)
                    sp.dma_start(rows_in[:, n], rows_in_dram[bass.ds(g, 1)].rearrange("n p c d -> (n p) c d")
                                 ).then_inc(s_rows_in[n], 16)

            def store_results(i):
                for n in range(2):
                    g = 2 * i + n
                    sp.wait_ge(s_rows_out, MOE_LOAD * (g + 1))
                    sp.dma_start(rows_out_dram[bass.ds(g, 1)].rearrange("n p c d -> (n p) c d"), rows_out[:, n]
                                 ).then_inc(s_results[n], 16)

            load_rows(0)
            with sp.Fori(0, ROW_TILES // MOE_BODY - 1) as i:
                load_rows(i + 1)
                store_results(i)
            store_results(ROW_TILES // MOE_BODY - 1)

            def store(b, n):
                sp.wait_ge(s_final, TILES * (b + 1))
                sp.dma_start(out_dram[bass.ds(b, 1)].rearrange("b p c d -> (b p) c d"), final[:, n]
                             ).then_inc(s_out[n], 16)

            for b in range(B):
                store(b, b % 2)
            for n in range(2):
                sp.wait_ge(s_out[n], 16 * ((B + 1 - n) // 2))

        @block.tensor
        def _(pe):
            pe.wait_ge(s_weights, WEIGHTS)
            for t in range(TAPS):
                pe.wait_ge(s_wtap, HALVES * (t + 1))
                if t >= 1:
                    pe.wait_ge(s_wconv, t)
                for c in range(HALVES):
                    mm = pe.matmul(l0_banks[:, 0, 0:2 * P], w_tap[:, c, :], pw[:, c, :],
                                   start=(c == 0), stop=(c == 1))
                mm.then_inc(s_wmul, 1)
            pe.wait_ge(s_wconv, TAPS)
            pe.wait_ge(s_prep, PREPARED)

            def fill(ring, use, it, *needs):
                drained(pe, ring, it, *(n for n in needs if ring.place[n][0] != ring.place[use][0]))
                after(pe, ring.free_sem(use), ring.free_at(use, it))
                return ring.bank(use), ring.full_sem(use)

            def turn(ring, use, src, it):
                bank, full = fill(ring, use, it)
                for t in range(TILES):
                    mm = pe.transpose(bank[:, t * P:(t + 1) * P], src[:, t, :], eye[:])
                mm.then_inc(full, 1)

            def layer0(u, i):
                if u == 0:
                    pe.wait_ge(s_x_loaded, at(i, 16, 16))
                    turn(l0, "xT", x_tok, i)
                if u == 1:
                    for h in range(HALVES):
                        bank, full = fill(l0, f"u{h}", i, "xT")
                        for t in range(TAPS):
                            mm = pe.matmul(bank, w_conv[:, t, h * P:(h + 1) * P], xT[:, t:t + T],
                                           start=(t == 0), stop=(t == TAPS - 1))
                        mm.then_inc(full, 1)
                if u == 2:
                    for h in range(HALVES):
                        bank, full = fill(l0, f"z{h}", i)
                        pe.matmul(bank, w_z[:, h * P:(h + 1) * P], xT[:, TAPS - 1:TAPS - 1 + T],
                                  start=True, stop=True).then_inc(full, 1)
                if u == 3:
                    pe.wait_ge(s_xc, at(i, HALVES, HALVES))
                    bank, full = fill(l0, "xdbl", i)
                    for h in range(HALVES):
                        mm = pe.matmul(bank[0:ROWS, :], w_x[:, h, :], xc[:, h, :], start=(h == 0), stop=(h == 1))
                    mm.then_inc(full, 1)
                if u == 4:
                    pe.wait_ge(s_dt_raw, at(i, 1, 1))
                    for h in range(HALVES):
                        bank, full = fill(l0, f"dt{h}", i)
                        pe.matmul(bank, w_dt[DT_ROW:DT_ROW + 8, h * P:(h + 1) * P],
                                  dt_raw[DT_ROW:DT_ROW + 8, :], start=True, stop=True).then_inc(full, 1)
                if 5 <= u < 5 + STATES:
                    n = u - 5
                    if n == 0:
                        pe.wait_ge(s_split, at(i, 4, 4))
                    for c, row in (("B", n), ("C", STATES + n)):
                        bank, full = fill(l0, f"{c}{n}", i)
                        pe.matmul(bank, sel[:, row, :], parts[:], start=True, stop=True).then_inc(full, 1)
                if u == 14:
                    pe.wait_ge(s_y, at(i, HALVES, HALVES))
                    bank, full = fill(l0, "mix", i)
                    for t in range(TILES):
                        for h in range(HALVES):
                            mm = pe.matmul(bank[:, t * P:(t + 1) * P], y[:, h, t * P:(t + 1) * P],
                                           w_out[:, h, :], start=(h == 0), stop=(h == 1))
                    mm.then_inc(full, 1)
                if u == 15:
                    pe.wait_ge(s_x1, at(i, TILES, TILES))
                    turn(l0, "x1T", x1, i)
                    bank, full = fill(l0, "ffn", i, "x1T")
                    for t in range(TILES):
                        mm = pe.matmul(bank[:, t * P:(t + 1) * P], x1T[:, t * P:(t + 1) * P], w_sign[:],
                                       start=True, stop=True)
                    mm.then_inc(full, 1)

            def opening(j):
                pe.wait_ge(s_x2_taken, at(j, 1, 1))
                turn(l1, "x2T", x3, j)
                bank, full = fill(l1, "wd", j, "x2T")
                pe.matmul(bank[0:ROWS, :], w_d[:], x2T[:], start=True, stop=True).then_inc(full, 1)

            def project(u, j):
                for name, w in (("q", w_q), ("g", w_g), ("k", w_k)):
                    bank, full = fill(l1, f"{name}{u}", j)
                    pe.matmul(bank, w[:, u * P:(u + 1) * P], x2T[:], start=True, stop=True).then_inc(full, 1)
                if u == 3:
                    pe.wait_ge(s_fall, at(j, TILES, TILES))
                    bank, full = fill(l1, "cpT", j)
                    for c in range(TILES):
                        mm = pe.transpose(bank[:, c * ROWS:(c + 1) * ROWS], fall[:, c * P:(c + 1) * P],
                                          eye[0:ROWS, 0:ROWS])
                    mm.then_inc(full, 1)
                if u == 5:
                    bank, full = fill(l1, "cpd", j, "cpT")
                    pe.matmul(bank[:, 0:TILES * HEADS], from_last[:], fall_tok[:], start=True, stop=True
                              ).then_inc(full, 1)

            def mask(g, c, j):
                bank, full = fill(l1, f"D{g}_{c}", j)
                here = slice(c * P, (c + 1) * P)
                pe.matmul(bank, fall_parts[:, here], sel[:, of_group(g), :], start=True, stop=False)
                pe.matmul(bank, eye_bf[:], future[:], start=False, stop=False)
                for h in range(4):
                    mm = pe.matmul(bank[:, h * P:(h + 1) * P], nsel[:, head_of(g, h), :], fall_parts[:, here],
                                   start=False, stop=(h == 3))
                mm.then_inc(full, 1)

            def scores(g, c, j):
                bank, full = fill(l1, f"S{g}_{c}", j)
                here = slice(c * P, (c + 1) * P)
                for h in range(4):
                    pair, rows = head_of(g, h) // 2, slice(g % 2 * DH, (g % 2 + 1) * DH)
                    mm = pe.matmul(bank[:, h * P:(h + 1) * P], k[rows, pair, here], q[rows, pair, here],
                                   start=True, stop=True)
                mm.then_inc(full, 1)

            def outputs(g, c, j):
                needs = [f"S{g}_{c}"]
                if g == 0:
                    needs += [f"v0_{c}", f"v1_{c}"] + ([f"U_{c - 1}"] if c else [])
                drained(pe, l1, j, *needs)
                if g % 2 == 0:
                    after(pe, s_osq, at(j, 2 * TILES, 2 * (c - 1) + g // 2 + 1))
                    after(pe, s_og, at(j, 2 * TILES, 2 * (c - 1) + g // 2 + 1))
                elif c:
                    pe.wait_ge(s_O, at(j, 4 * TILES, 4 * c + g))
                if g == 0:
                    pe.wait_ge(s_qd, at(j, TILES, c + 1))
                for h in range(4):
                    head = head_of(g, h)
                    pair, rows = head // 2, slice(g % 2 * DH, (g % 2 + 1) * DH)
                    to = o_banks[:, g // 2, head % 8 * DH:(head % 8 + 1) * DH]
                    mm = pe.matmul(to, S[:, g % 2, h * P:(h + 1) * P], v[:, head * DH:(head + 1) * DH],
                                   start=True, stop=(c == 0))
                    if c:
                        mm = pe.matmul(to, qd[rows, pair, :], state[rows, pair, :], start=False, stop=True)
                mm.then_inc(s_O, 1)

            def update(c, j):
                bank, full = fill(l1, f"U_{c}", j, f"kT0_{c}", f"kT1_{c}")
                for head in range(HEADS):
                    rows = slice(head % 2 * DH, (head % 2 + 1) * DH)
                    mm = pe.matmul(bank[rows, head // 2 * DH:(head // 2 + 1) * DH], kd[:, head, :],
                                   v[:, head * DH:(head + 1) * DH], start=True, stop=True)
                mm.then_inc(full, 1)

            def turn_out(c, j):
                for f in range(2):
                    pe.wait_ge(s_og, at(j, 2 * TILES, 2 * c + f + 1))
                    bank, full = fill(l1, f"OT{f}_{c}", j)
                    for t in range(4):
                        mm = pe.transpose(bank[:, t * P:(t + 1) * P], o[:, (4 * f + t) * P:(4 * f + t + 1) * P],
                                          eye[:])
                    mm.then_inc(full, 1)

            def project_out(c, j):
                bank, full = fill(l1, f"wo_{c}", j, f"OT0_{c}", f"OT1_{c}")
                for t in range(PAIRS):
                    mm = pe.matmul(bank[:, 0:P], oT[:, t, :], w_o[:, t, :], start=(t == 0), stop=(t == PAIRS - 1))
                mm.then_inc(full, 1)

            def half_chunk(u, j):
                c, f = divmod(u - PAIRS, 2)
                here = slice(c * P, (c + 1) * P)
                if f == 0:
                    for name, w in (("v", w_v), ("o", w_og)):
                        for n in range(2):
                            bank, full = fill(l1, f"{name}{n}_{c}", j)
                            pe.matmul(bank, x2T[:, here], w[:, n * T:(n + 1) * T], start=True, stop=True
                                      ).then_inc(full, 1)
                    if c == 0:
                        pe.wait_ge(s_fsplit, at(j, 5, 5))
                    for n in range(2):
                        all_keys = [f"{m}{p}" for p in range(PAIRS) for m in "qk"] if c == 0 and n == 0 else []
                        bank, full = fill(l1, f"e{n}_{c}", j, *all_keys)
                        for t in range(4):
                            mm = pe.matmul(bank[:, t * P:(t + 1) * P], nselpair[:, 4 * n + t, :],
                                           fall_parts[:, here], start=True, stop=True)
                        mm.then_inc(full, 1)
                    for n in range(2):
                        bank, full = fill(l1, f"kT{n}_{c}", j)
                        for t in range(4):
                            mm = pe.transpose(bank[:, t * P:(t + 1) * P], k[:, 4 * n + t, here], eye[:])
                        mm.then_inc(full, 1)
                    mask(0, c, j)
                    scores(0, c, j)
                    if c:
                        turn_out(c - 1, j)
                    mask(1, c, j)
                    scores(1, c, j)
                    if c:
                        project_out(c - 1, j)
                    outputs(0, c, j)
                else:
                    mask(2, c, j)
                    scores(2, c, j)
                    outputs(1, c, j)
                    mask(3, c, j)
                    scores(3, c, j)
                    outputs(2, c, j)
                    outputs(3, c, j)
                    if c < TILES - 1:
                        update(c, j)

            def closing(j):
                turn_out(TILES - 1, j)
                project_out(TILES - 1, j)
                pe.wait_ge(s_x3, at(j, TILES, TILES))
                turn(l1, "x3T", x3, j)
                bank, full = fill(l1, "route", j, "x3T")
                for t in range(TILES):
                    mm = pe.matmul(bank[:, t * EXPERTS:(t + 1) * EXPERTS], x3T[:, t * P:(t + 1) * P], w_route[:],
                                   start=True, stop=True)
                mm.then_inc(full, 1)

            def body(i, j):
                if j is not None:
                    opening(j)
                for u in range(UNITS):
                    if j is not None:
                        project(u, j) if u < PAIRS else half_chunk(u, j)
                    if i is not None:
                        layer0(u, i)
                if j is not None:
                    closing(j)

            rounds(pe, body)

            pe.wait_ge(s_route, ROUTE_HOT)
            drained(pe, l1, B - 1, "route")
            pe.matmul(l1_banks[:, 0, 0:TOK_TILES * EXPERTS], earlier[:], hot_bf[:], start=True, stop=True)
            pe.matmul(l1_banks[:, 1, 0:TOK_TILES * EXPERTS], ones_bf[:], hot_bf[:], start=True, stop=True
                      ).then_inc(s_counted, 1)

            def turn_rows(i, n):
                g = 2 * i + n
                pe.wait_ge(s_rows_in[n], at(i, 16, 16))
                after(pe, s_rowsT, g)
                for t in range(MOE_LOAD):
                    mm = pe.transpose(bank_rows[:, t * P:(t + 1) * P], rows_in[:, n, t, :], eye[:])
                mm.then_inc(s_turned, 1)

            def expert_of(t):
                return pe.value_load(expert_i[0:1, bass.ds(t, 1)], min_val=0, max_val=EXPERTS - 1)

            def hidden(t, u):
                e = expert_of(t)
                if u % MOE_LOAD == 0:
                    pe.wait_ge(s_rowsT, t // MOE_LOAD + 1 if isinstance(t, int) else (t - u) // MOE_LOAD + u // MOE_LOAD + 1)
                after(pe, s_act_h, t - 1)
                n = u // MOE_LOAD
                x = rowsT[:, n, u % MOE_LOAD * P:(u % MOE_LOAD + 1) * P]
                pe.matmul(bank_h[:, u % 2, 0, :], x, w_0[:, bass.ds(e * FF, FF)], start=True, stop=True)
                pe.matmul(bank_h[:, u % 2, 1, :], x, w_1[:, bass.ds(e * FF, FF)], start=True, stop=True
                          ).then_inc(s_h, 1)

            def turn_hidden(t, u):
                pe.wait_ge(s_act_h, t + 1)
                after(pe, s_hT, t - 1)
                for f in range(FCHUNKS):
                    mm = pe.transpose(bank_hT[:, u % 2, f * P:(f + 1) * P], act_h[:, u % 2, f * P:(f + 1) * P], eye[:])
                mm.then_inc(s_h_turned, 1)

            def results(t, u):
                e = expert_of(t)
                pe.wait_ge(s_hT, t + 1)
                after(pe, s_rows_out, t)
                for f in range(FCHUNKS):
                    mm = pe.matmul(bank_y[:, 0:P], hT[:, u % 2, f * P:(f + 1) * P],
                                   w_2[:, bass.ds(e * FF + f * P, P)], start=(f == 0), stop=(f == FCHUNKS - 1))
                mm.then_inc(s_y_tile, 1)

            pe.wait_ge(s_w_moe, 16 * 3)
            pe.wait_ge(s_expert, 1)
            pe.wait_ge(s_route, ROUTE_TAKEN)

            def experts(i):
                for u in range(MOE_BODY):
                    t = i * MOE_BODY + u
                    if u % MOE_LOAD == 0:
                        turn_rows(i, u // MOE_LOAD)
                    hidden(t, u)
                    if u >= 1 or not first(i):
                        turn_hidden(t - 1, (u - 1) % MOE_BODY)
                    if u >= 2 or not first(i):
                        results(t - 2, (u - 2) % MOE_BODY)

            experts(0)
            with pe.Fori(1, ROW_TILES // MOE_BODY) as i:
                experts(i)
            turn_hidden(ROW_TILES - 1, MOE_BODY - 1)
            results(ROW_TILES - 2, MOE_BODY - 2)
            results(ROW_TILES - 1, MOE_BODY - 1)

        @block.scalar
        def _(act):
            act.wait_ge(s_weights, WEIGHTS)
            nc.scalar.activation(a_neg[:], a_log[:], ACT.Exp).then_inc(s_alog, 1)
            for t in range(TAPS):
                act.wait_ge(s_wmul, t + 1)
                nc.scalar.activation(w_conv[:, t, :], l0_banks[:, 0, 0:2 * P], ACT.Copy, scale=0.5
                                     ).then_inc(s_wconv, 1)

            def full(ring, use, it):
                act.wait_ge(ring.full_sem(use), ring.full_at(use, it))
                return ring.bank(use)

            def layer0(u, i):
                if u == 0:
                    nc.scalar.copy(xT[:, TAPS - 1:TAPS - 1 + T], full(l0, "xT", i)).then_inc(l0.free_sem("xT"), 1)
                if u == 1:
                    for h in range(HALVES):
                        if h == 0:
                            after(act, s_du, at(i, 1, 0))
                            after(act, s_y, at(i, HALVES, 0))
                        nc.scalar.activation(xc[:, h, :], full(l0, f"u{h}", i), ACT.Identity,
                                             bias=b_conv[:, h:h + 1]).then_inc(l0.free_sem(f"u{h}"), 1)
                        drained(act, l0, i, f"u{h}")
                        nc.scalar.activation(th[:, h, :], xc[:, h, :], ACT.Tanh).then_inc(s_tanh, 1)
                if u == 2:
                    for h in range(HALVES):
                        bank = full(l0, f"z{h}", i)
                        act.wait_ge(s_xc, at(i, HALVES, h + 1))
                        nc.scalar.activation(th[:, h, :], bank, ACT.Tanh, scale=0.5).then_inc(s_tanh, 1)
                if u == 3:
                    nc.scalar.copy(dt_raw[DT_ROW:DT_ROW + 8, :], full(l0, "xdbl", i)[DT_ROW:DT_ROW + 8, :]
                                   ).then_inc(s_dt_raw, 1)
                if u == 4:
                    for h in range(HALVES):
                        nc.scalar.activation(delta[:, h, :], full(l0, f"dt{h}", i), ACT.Identity,
                                             bias=b_dt[:, h:h + 1]).then_inc(l0.free_sem(f"dt{h}"), 1)
                    drained(act, l0, i, "z0", "z1", "dt0", "dt1")
                    nc.scalar.activation(th[:], delta[:], ACT.Abs).then_inc(s_sp, 1)
                    act.wait_ge(s_sp, at(i, 3, 1))
                    nc.scalar.activation(th[:], th[:], ACT.Exp, scale=-1.0).then_inc(s_sp, 1)
                    act.wait_ge(s_sp, at(i, 3, 2))
                    nc.scalar.activation(th[:], th[:], ACT.Ln, bias=1.0).then_inc(s_sp, 1)
                if 5 <= u < 5 + STATES:
                    n = u - 5
                    if n == 0:
                        act.wait_ge(s_delta, at(i, HALVES, HALVES))
                    after(act, s_scan, at(i, 2 * STATES, 2 * (n - 1)))
                    for h in range(HALVES):
                        nc.scalar.activation(decay[:, n % 2, h, :], delta[:, h, :], ACT.Exp,
                                             scale=a_neg[:, h, n:n + 1]).then_inc(s_decay, 1)
                if u == 15:
                    nc.scalar.copy(x1T[:], full(l0, "x1T", i)).then_inc(l0.free_sem("x1T"), 1)

            def opening(j):
                nc.scalar.copy(x2T[:], full(l1, "x2T", j)).then_inc(l1.free_sem("x2T"), 1)
                nc.scalar.activation(sp_in[:], full(l1, "wd", j)[0:ROWS, :], ACT.Identity, bias=b_d[:]
                                     ).then_inc(l1.free_sem("wd"), 1)
                drained(act, l1, j, "wd")
                nc.scalar.activation(sp_ln[:], sp_in[:], ACT.Abs).then_inc(s_dsp, 1)
                act.wait_ge(s_dsp, at(j, 3, 1))
                nc.scalar.activation(sp_ln[:], sp_ln[:], ACT.Exp, scale=-1.0).then_inc(s_dsp, 1)
                act.wait_ge(s_dsp, at(j, 3, 2))
                nc.scalar.activation(sp_ln[:], sp_ln[:], ACT.Ln, bias=1.0).then_inc(s_dsp, 1)

            def drain(dst, use, j, func=ACT.Copy, scale=1.0):
                nc.scalar.activation(dst, full(l1, use, j), func, scale=scale).then_inc(l1.free_sem(use), 1)

            def project(u, j):
                if u == 0 and first(j):
                    act.wait_ge(s_cleared, 16 * (ROW_TILES // ZERO_ROWS))
                drain(q[:, u, :], f"q{u}", j)
                if u >= 2:
                    drained(act, l1, j, f"k{u - 2}")
                drain(tg[:, u % 2, :], f"g{u}", j, ACT.Tanh, 0.5)
                if u == 3:
                    nc.scalar.copy(fall_tok[:].rearrange("p (c h) -> p c h", h=HEADS),
                                   full(l1, "cpT", j)[:, 0:TILES * ROWS].rearrange("p (c r) -> p c r", r=ROWS)[:, :, 0:HEADS]
                                   ).then_inc(l1.free_sem("cpT"), 1)
                if u == 5:
                    nc.scalar.activation(to_end[:], full(l1, "cpd", j)[:, 0:TILES * HEADS].rearrange(
                        "p (c h) -> p c h", h=HEADS), ACT.Exp).then_inc(l1.free_sem("cpd"), 1)

            def decay_mask(g, c, j):
                if g >= 2 or c:
                    drained(act, l1, j, f"S{(g + 2) % 4}_{c if g >= 2 else c - 1}")
                nc.scalar.activation(E[:, g % 2, :], full(l1, f"D{g}_{c}", j), ACT.Exp).then_inc(l1.free_sem(f"D{g}_{c}"), 1)

            def squares(f, c, j):
                act.wait_ge(s_O, at(j, 4 * TILES, 4 * c + 2 * f + 2))
                after(act, s_osq, at(j, 2 * TILES, 2 * c + f))
                nc.scalar.activation(sq[:], o_banks[:, f, :], ACT.Square, accum_out=ssq[:, c, f:f + 1]
                                     ).then_inc(s_osq, 1)

            def turned_out(c, j):
                for f in range(2):
                    nc.scalar.activation(oT[:, 4 * f:4 * f + 4, :],
                                         full(l1, f"OT{f}_{c}", j).rearrange("p (t n) -> p t n", n=P), ACT.Copy
                                         ).then_inc(l1.free_sem(f"OT{f}_{c}"), 1)

            def half_chunk(u, j):
                c, f = divmod(u - PAIRS, 2)
                if f == 0:
                    for n in range(2):
                        drain(v[:, n * T:(n + 1) * T], f"v{n}_{c}", j)
                    after(act, s_og, at(j, 2 * TILES, 2 * c))
                    for n in range(2):
                        drain(tog[:, n * T:(n + 1) * T], f"o{n}_{c}", j, ACT.Tanh, 0.5)
                    after(act, s_qd, at(j, TILES, c))
                    after(act, s_decst, at(j, TILES - 2, max(c - 1, 0)))
                    for n in range(2):
                        nc.scalar.activation(from_start[:, 4 * n:4 * n + 4, :],
                                             full(l1, f"e{n}_{c}", j).rearrange("p (t n) -> p t n", n=P), ACT.Exp
                                             ).then_inc(l1.free_sem(f"e{n}_{c}"), 1)
                    decay_mask(0, c, j)
                    if c:
                        turned_out(c - 1, j)
                    decay_mask(1, c, j)
                else:
                    decay_mask(2, c, j)
                    squares(0, c, j)
                    decay_mask(3, c, j)
                    squares(1, c, j)

            def closing(j):
                turned_out(TILES - 1, j)
                drain(x3T[:], "x3T", j)
                nc.scalar.copy(logits[:, bass.ds(j * TILES, TILES), :],
                               full(l1, "route", j)[:, 0:TILES * EXPERTS].rearrange("p (t e) -> p t e", e=EXPERTS)
                               ).then_inc(l1.free_sem("route"), 1)

            def body(i, j):
                if j is not None:
                    opening(j)
                for u in range(UNITS):
                    if j is not None:
                        project(u, j) if u < PAIRS else half_chunk(u, j)
                    if i is not None:
                        layer0(u, i)
                if j is not None:
                    closing(j)

            rounds(act, body)

            act.wait_ge(s_route, ROUTE_BEST)
            nc.scalar.activation(share[:, 1, :], share[:, 0, :], ACT.Exp).then_inc(s_share, 1)

            def turned_rows(i, n):
                g = 2 * i + n
                act.wait_ge(s_turned, g + 1)
                after(act, s_h, MOE_LOAD * (g - 1) if not first(i) else 0)
                nc.scalar.copy(rowsT[:, n, :], bank_rows).then_inc(s_rowsT, 1)

            def tanh_hidden(t, u):
                act.wait_ge(s_h, t + 1)
                after(act, s_silu, t - 1)
                nc.scalar.activation(tanh_h[:, u % 2, :], bank_h[:, u % 2, 0, :], ACT.Tanh, scale=0.5
                                     ).then_inc(s_tanh_h, 1)

            def turned_hidden(t, u):
                act.wait_ge(s_h_turned, t + 1)
                after(act, s_y_tile, t - 1)
                nc.scalar.copy(hT[:, u % 2, :], bank_hT[:, u % 2, :]).then_inc(s_hT, 1)

            def result_out(t, u):
                act.wait_ge(s_y_tile, t + 1)
                if u % MOE_LOAD == 0 and not first_pass(t, u):
                    act.wait_ge(s_results[u // MOE_LOAD], stored_before(t, u))
                nc.scalar.copy(rows_out[:, u // MOE_LOAD, u % MOE_LOAD, :], bank_y[:, 0:P]).then_inc(s_rows_out, 1)

            def first_pass(t, u):
                return isinstance(t, int) and t < MOE_BODY

            def stored_before(t, u):
                return 2 * (t - u)

            def experts(i):
                for u in range(MOE_BODY):
                    t = i * MOE_BODY + u
                    if u % MOE_LOAD == 0:
                        turned_rows(i, u // MOE_LOAD)
                    tanh_hidden(t, u)
                    if u >= 1 or not first(i):
                        turned_hidden(t - 1, (u - 1) % MOE_BODY)
                    if u >= 2 or not first(i):
                        result_out(t - 2, (u - 2) % MOE_BODY)

            experts(0)
            with act.Fori(1, ROW_TILES // MOE_BODY) as i:
                experts(i)
            turned_hidden(ROW_TILES - 1, MOE_BODY - 1)
            result_out(ROW_TILES - 2, MOE_BODY - 2)
            result_out(ROW_TILES - 1, MOE_BODY - 1)

        @block.vector
        def _(dve):
            nc.vector.memset(xT[:, 0:TAPS - 1], 0.0).then_inc(s_prep, 1)
            nc.vector.memset(ones[:], 1.0).then_inc(s_prep, 1)
            nc.vector.memset(zeros, 0.0).then_inc(s_zero, 1)
            dve.wait_ge(s_weights, WEIGHTS)
            for t in range(TAPS):
                if t >= 1:
                    dve.wait_ge(s_wmul, t)
                for c in range(HALVES):
                    nc.vector.tensor_scalar(w_tap[:, c, :], w_inT[:, c, :], taps[:, c, t:t + 1], None,
                                            ALU.mult).then_inc(s_wtap, 1)
            for w in (b_conv, w_out, w_k):
                nc.vector.tensor_scalar(w[:], w[:], 0.5, None, ALU.mult).then_inc(s_prep, 1)
            for t in range(PAIRS):
                nc.vector.tensor_scalar(w_o[:, t, :], w_o[:, t, :], norm_w[:, t:t + 1], 0.5 * HID ** 0.5, ALU.mult, ALU.mult
                                        ).then_inc(s_prep, 1)
            nc.vector.tensor_scalar(w_less[:], w_ffn[:], 0.0, None, ALU.is_lt).then_inc(s_sign, 1)
            nc.vector.tensor_scalar(w_sign[:], w_ffn[:], 0.0, None, ALU.is_gt).then_inc(s_sign, 1)
            dve.wait_ge(s_sign, 2)
            nc.vector.tensor_tensor(w_sign[:], w_sign[:], w_less[:], ALU.subtract).then_inc(s_prep, 1)
            dve.wait_ge(s_alog, 1)
            nc.vector.tensor_scalar(a_neg[:], a_neg[:], -1.0, None, ALU.mult).then_inc(s_prep, 1)
            dve.wait_ge(s_prep, PREPARED)

            def full(ring, use, it):
                dve.wait_ge(ring.full_sem(use), ring.full_at(use, it))
                return ring.bank(use)

            def split(ps, rs, step, base, per, it):
                dve.wait_ge(step, at(it, per, base))
                nc.vector.tensor_copy(ps[PART2:ROWS, :], rs[PART2:ROWS, :]).then_inc(step, 1)
                dve.wait_ge(step, at(it, per, base + 1))
                nc.vector.tensor_tensor(rs[PART3:ROWS, :], rs[PART3:ROWS, :], ps[PART3:ROWS, :], ALU.subtract
                                        ).then_inc(step, 1)
                dve.wait_ge(step, at(it, per, base + 2))
                nc.vector.tensor_copy(ps[PART3:ROWS, :], rs[PART3:ROWS, :]).then_inc(step, 1)

            def layer_norm(x, step, scale, done, it):
                for t in range(TILES):
                    nc.vector.bn_stats(stats[:, t, :], x[:, t, :]).then_inc(step, 1)
                dve.wait_ge(step, at(it, LN_STEPS, 4))
                nc.vector.tensor_tensor(mean[:], stats[:, :, 1], stats[:, :, 4], ALU.add).then_inc(step, 1)
                nc.vector.tensor_tensor(apart[:], stats[:, :, 1], stats[:, :, 4], ALU.subtract).then_inc(step, 1)
                nc.vector.tensor_tensor(var[:], stats[:, :, 2], stats[:, :, 5], ALU.add).then_inc(step, 1)
                dve.wait_ge(step, at(it, LN_STEPS, 6))
                nc.vector.tensor_tensor(apart[:], apart[:], apart[:], ALU.mult).then_inc(step, 1)
                nc.vector.tensor_scalar(mean[:], mean[:], 0.5, None, ALU.mult).then_inc(step, 1)
                dve.wait_ge(step, at(it, LN_STEPS, 8))
                nc.vector.scalar_tensor_tensor(var[:], apart[:], P / 4, var[:], ALU.mult, ALU.add).then_inc(step, 1)
                dve.wait_ge(step, at(it, LN_STEPS, 10))
                nc.vector.tensor_scalar(var[:], var[:], 1 / P, LN_EPS, ALU.mult, ALU.add).then_inc(step, 1)
                dve.wait_ge(scale, at(it, 1, 1))
                for t in range(TILES):
                    nc.vector.tensor_scalar(x[:, t, :], x[:, t, :], mean[:, t:t + 1], rstd[:, t:t + 1],
                                            ALU.subtract, ALU.mult).then_inc(done, 1)

            def layer0(u, i):
                if u == 1:
                    for h in range(HALVES):
                        dve.wait_ge(s_tanh, at(i, 4, h + 1))
                        nc.vector.scalar_tensor_tensor(xc[:, h, :], th[:, h, :], 1.0, xc[:, h, :],
                                                       ALU.add, ALU.mult).then_inc(s_xc, 1)
                if u == 2:
                    for h in range(HALVES):
                        dve.wait_ge(s_tanh, at(i, 4, 3 + h))
                        nc.vector.scalar_tensor_tensor(sz[:, h, :], th[:, h, :], 1.0, full(l0, f"z{h}", i),
                                                       ALU.add, ALU.mult).then_inc(l0.free_sem(f"z{h}"), 1)
                if u == 3:
                    bank = full(l0, "xdbl", i)[0:ROWS, :]
                    dve.wait_ge(s_dt_raw, at(i, 1, 1))
                    nc.vector.tensor_copy(parts[:], bank).then_inc(s_split, 1)
                    dve.wait_ge(s_split, at(i, 4, 1))
                    nc.vector.tensor_tensor(rest[:], bank, parts[:], ALU.subtract).then_inc(l0.free_sem("xdbl"), 1)
                    drained(dve, l0, i, "xdbl")
                    split(parts, rest, s_split, 1, 4, i)
                if u == 4:
                    dve.wait_ge(s_sp, at(i, 3, 3))
                    for h in range(HALVES):
                        nc.vector.scalar_tensor_tensor(delta[:, h, :], delta[:, h, :], 0.0, th[:, h, :],
                                                       ALU.max, ALU.add).then_inc(s_delta, 1)
                    dve.wait_ge(s_delta, at(i, HALVES, HALVES))
                    nc.vector.tensor_tensor(du[:], delta[:], xc[:], ALU.mult).then_inc(s_du, 1)
                if 5 <= u < 5 + STATES:
                    n = u - 5
                    if n == 0:
                        dve.wait_ge(s_du, at(i, 1, 1))
                    after(dve, s_scan, at(i, 2 * STATES, 2 * n))
                    both = full(l0, f"B{n}", i).unsqueeze(1).broadcast_to([P, HALVES, T])
                    nc.vector.tensor_tensor(push[:], du[:], both, ALU.mult).then_inc(l0.free_sem(f"B{n}"), 1)
                    drained(dve, l0, i, f"B{n}")
                    if n:
                        drained(dve, l0, i, f"C{n - 1}")
                    for h in range(HALVES):
                        dve.wait_ge(s_decay, at(i, 2 * STATES, 2 * n + h + 1))
                        nc.vector.tensor_tensor_scan(hs[:, h, :], decay[:, n % 2, h, :], push[:, h, :], 0.0,
                                                     ALU.mult, ALU.add).then_inc(s_scan, 1)
                    both = full(l0, f"C{n}", i).unsqueeze(1).broadcast_to([P, HALVES, T])
                    dve.wait_ge(s_scan, at(i, 2 * STATES, 2 * n + 2))
                    after(dve, s_ysum, at(i, STATES - 1, 0 if n < 2 else max(n - 2, 1)))
                    nc.vector.tensor_tensor(ch[:, n % 2, :, :], hs[:], both, ALU.mult).then_inc(l0.free_sem(f"C{n}"), 1)
                if u == 13:
                    dve.wait_ge(s_ysum, at(i, STATES - 1, STATES - 1))
                    for h in range(HALVES):
                        nc.vector.scalar_tensor_tensor(y[:, h, :], xc[:, h, :], d_skip[:, h:h + 1], y[:, h, :],
                                                       ALU.mult, ALU.add).then_inc(s_ygate, 1)
                    for h in range(HALVES):
                        dve.wait_ge(s_ygate, at(i, HALVES, h + 1))
                        nc.vector.tensor_tensor(y[:, h, :], y[:, h, :], sz[:, h, :], ALU.mult).then_inc(s_y, 1)
                if u == 14:
                    dve.wait_ge(s_x_loaded, at(i, 16, 16))
                    nc.vector.tensor_tensor(x1[:], full(l0, "mix", i).rearrange("p (t d) -> p t d", d=P), x_tok[:],
                                            ALU.add).then_inc(l0.free_sem("mix"), 1)
                    drained(dve, l0, i, "mix")
                    layer_norm(x1, s_ln0, s_rstd0, s_x1, i)
                if u == 15:
                    after(dve, s_x2_taken, at(i, 1, 0))
                    nc.vector.tensor_tensor(x2_new[:], full(l0, "ffn", i).rearrange("p (t d) -> p t d", d=P), x1[:],
                                            ALU.add).then_inc(l0.free_sem("ffn"), 1)
                    drained(dve, l0, i, "ffn")
                    layer_norm(x2_new, s_ln1, s_rstd1, s_x2, i)

            def opening(j):
                dve.wait_ge(s_x2, at(j, TILES, TILES))
                if not first(j):
                    dve.wait_ge(s_x3_stored, at(j, 16, 0))
                    dve.wait_ge(l1.full_sem("x3T"), l1.full_at("x3T", j - 1))
                nc.vector.tensor_copy(x3[:], x2_new[:]).then_inc(s_x2_taken, 1)
                dve.wait_ge(s_dsp, at(j, 3, 3))
                nc.vector.scalar_tensor_tensor(sp_in[:], sp_in[:], 0.0, sp_ln[:], ALU.max, ALU.add).then_inc(s_dlog, 1)
                dve.wait_ge(s_dlog, at(j, 1, 1))
                for c in range(TILES):
                    here = slice(c * P, (c + 1) * P)
                    nc.vector.tensor_tensor_scan(fall[:, here], ones[:], sp_in[:, here], 0.0,
                                                 ALU.mult, ALU.add).then_inc(s_fall, 1)
                dve.wait_ge(s_fall, at(j, TILES, TILES))
                nc.vector.tensor_copy(fall_parts[:], fall[:]).then_inc(s_fsplit, 1)
                dve.wait_ge(s_fsplit, at(j, 5, 1))
                nc.vector.tensor_tensor(fall_rest[:], fall[:], fall_parts[:], ALU.subtract).then_inc(s_fsplit, 1)
                split(fall_parts, fall_rest, s_fsplit, 2, 5, j)

            def project(u, j):
                drained(dve, l1, j, f"g{u}")
                nc.vector.scalar_tensor_tensor(k[:, u, :], tg[:, u % 2, :], 1.0, full(l1, f"k{u}", j),
                                               ALU.add, ALU.mult).then_inc(l1.free_sem(f"k{u}"), 1)

            def mask_scores(g, c, j):
                drained(dve, l1, j, f"D{g}_{c}")
                nc.vector.tensor_tensor(S[:, g % 2, :], full(l1, f"S{g}_{c}", j), E[:, g % 2, :], ALU.mult
                                        ).then_inc(l1.free_sem(f"S{g}_{c}"), 1)

            def gate_out(f, c, j):
                dve.wait_ge(s_O, at(j, 4 * TILES, 4 * c + 2 * f + 2))
                drained(dve, l1, j, f"o{f}_{c}")
                dve.wait_ge(s_osq, at(j, 2 * TILES, 2 * c + f + 1))
                nc.vector.scalar_tensor_tensor(o[:, f * T:(f + 1) * T], tog[:, f * T:(f + 1) * T], 1.0,
                                               o_banks[:, f, :], ALU.add, ALU.mult).then_inc(s_og, 1)

            def residual(c, j):
                dve.wait_ge(s_osq, at(j, 2 * TILES, 2 * c + 2))
                nc.vector.tensor_tensor(rms[:, c:c + 1], ssq[:, c, 0:1], ssq[:, c, 1:2], ALU.add).then_inc(s_rms, 1)
                dve.wait_ge(s_rms_pow, at(j, TILES, c + 1))
                nc.vector.scalar_tensor_tensor(x3[:, c, :], full(l1, f"wo_{c}", j)[:, 0:P], rms[:, c:c + 1],
                                               x3[:, c, :], ALU.mult, ALU.add).then_inc(l1.free_sem(f"wo_{c}"), 1)

            def half_chunk(u, j):
                c, f = divmod(u - PAIRS, 2)
                if f == 0:
                    if c == 0:
                        drained(dve, l1, j, "cpd")
                    for n in range(2):
                        heads = slice(8 * n, 8 * n + 8)
                        nc.vector.tensor_tensor(
                            kd[:, heads, :], full(l1, f"kT{n}_{c}", j).rearrange("p (h d) -> p h d", d=DH),
                            to_end[:, c, heads].unsqueeze(2).broadcast_to([P, 8, DH]), ALU.mult
                        ).then_inc(l1.free_sem(f"kT{n}_{c}"), 1)
                    mask_scores(0, c, j)
                    mask_scores(1, c, j)
                    if c:
                        residual(c - 1, j)
                else:
                    mask_scores(2, c, j)
                    gate_out(0, c, j)
                    mask_scores(3, c, j)
                    gate_out(1, c, j)
                    if c < TILES - 1:
                        new = full(l1, f"U_{c}", j).rearrange("p (h d) -> p h d", d=DH)
                        if c == 0:
                            nc.vector.tensor_copy(state[:], new).then_inc(l1.free_sem(f"U_{c}"), 1)
                        else:
                            drained(dve, l1, j, f"U_{c - 1}")
                            nc.vector.tensor_tensor(state[:], state[:],
                                                    from_start[:, :, P - 1:P].broadcast_to([P, PAIRS, DH]), ALU.mult
                                                    ).then_inc(s_decst, 1)
                            dve.wait_ge(s_decst, at(j, TILES - 2, c))
                            nc.vector.tensor_tensor(state[:], state[:], new, ALU.add).then_inc(l1.free_sem(f"U_{c}"), 1)

            def closing(j):
                residual(TILES - 1, j)
                drained(dve, l1, j, *(f"wo_{c}" for c in range(TILES)))
                layer_norm(x3, s_ln3, s_rstd3, s_x3, j)

            def body(i, j):
                if j is not None:
                    opening(j)
                for u in range(UNITS):
                    if j is not None:
                        project(u, j) if u < PAIRS else half_chunk(u, j)
                    if i is not None:
                        layer0(u, i)
                if j is not None:
                    closing(j)

            rounds(dve, body)

            attention_over(dve)
            dve.wait_ge(s_x3_stored, 16 * B)
            wide = [P, TOK_TILES, EXPERTS]
            steps = [0]

            def step(ins):
                steps[0] += 1
                ins.then_inc(s_route, 1)
                dve.wait_ge(s_route, steps[0])

            def each(x):
                return x.unsqueeze(2).broadcast_to(wide)

            rev_all = rev[:].unsqueeze(1).broadcast_to(wide)
            source = logits
            for n in range(2):
                step(nc.vector.tensor_reduce(best[:, n, :], source[:], AX.X, ALU.max))
                step(nc.vector.tensor_tensor(hot[:, n], source[:], each(best[:, n, :]), ALU.is_equal))
                step(nc.vector.tensor_tensor(hot[:, n], hot[:, n], rev_all, ALU.mult))
                step(nc.vector.tensor_reduce(place[:, n, :], hot[:, n], AX.X, ALU.max))
                step(nc.vector.tensor_tensor(hot[:, n], rev_all, each(place[:, n, :]), ALU.is_equal))
                if n == 0:
                    step(nc.vector.scalar_tensor_tensor(work[:], hot[:, 0], -3e38, logits[:], ALU.mult, ALU.add))
                    source = work
            step(nc.vector.tensor_tensor(hot_bf[:], hot[:, 0], hot[:, 1], ALU.add))
            assert steps[0] == ROUTE_HOT
            step(nc.vector.tensor_tensor(share[:, 0, :], best[:, 1, :], best[:, 0, :], ALU.subtract))
            assert steps[0] == ROUTE_BEST
            step(nc.vector.memset(ones_r[:], 1.0))
            dve.wait_ge(s_counted, 1)
            count = [P, TOK_TILES * EXPERTS]
            step(nc.vector.tensor_copy(rank[:], l1_banks[:, 0, 0:count[1]].rearrange("p (t e) -> p t e", e=EXPERTS)))
            step(nc.vector.tensor_copy(total[:], l1_banks[:, 1, 0:count[1]].rearrange("p (t e) -> p e t", e=EXPERTS)))
            assert steps[0] == ROUTE_TAKEN
            for e in range(EXPERTS):
                step(nc.vector.tensor_tensor_scan(upto[:, e, :], ones_r[:], total[:, e, :], 0.0, ALU.mult, ALU.add))
            step(nc.vector.tensor_scalar(count_i[:], upto[:, :, TOK_TILES - 1], float(P - 1), None, ALU.add))
            step(nc.vector.tensor_scalar(count_i[:], count_i[:], 7, None, ALU.arith_shift_right))
            step(nc.vector.tensor_copy(tiles_of[:], count_i[:]))
            step(nc.vector.tensor_tensor_scan(ends[:], ones_r[:, 0:EXPERTS], tiles_of[:], 0.0, ALU.mult, ALU.add))
            step(nc.vector.tensor_tensor(base[:], ends[:], tiles_of[:], ALU.subtract))
            step(nc.vector.tensor_scalar(base[:], base[:], float(P), None, ALU.mult))
            step(nc.vector.tensor_tensor(upto[:], upto[:], total[:], ALU.subtract))
            step(nc.vector.tensor_tensor(upto[:], upto[:], base[:].unsqueeze(2).broadcast_to([P, EXPERTS, TOK_TILES]),
                                         ALU.add))
            step(nc.vector.tensor_tensor(rank[:], rank[:], upto[:].rearrange("p e t -> p t e"), ALU.add))
            for n in range(2):
                step(nc.vector.tensor_tensor(work[:], rank[:], hot[:, n], ALU.mult))
                step(nc.vector.tensor_reduce(place[:, n, :], work[:], AX.X, ALU.add))
            nc.vector.tensor_copy(row_of[:], place[:]).then_inc(s_rows_known, 1)
            step(nc.vector.tensor_tensor(past[:], tile_no[:].unsqueeze(2).broadcast_to([1, ROW_TILES, EXPERTS]),
                                         ends[0:1, :].unsqueeze(1).broadcast_to([1, ROW_TILES, EXPERTS]), ALU.is_ge))
            step(nc.vector.tensor_reduce(expert_f[:], past[:], AX.X, ALU.add))
            step(nc.vector.tensor_scalar(expert_f[:], expert_f[:], float(EXPERTS - 1), None, ALU.min))
            nc.vector.tensor_copy(expert_i[:], expert_f[:]).then_inc(s_expert, 1)
            dve.wait_ge(s_share, 1)
            step(nc.vector.tensor_scalar(share[:, 0, :], share[:, 1, :], 2.0, 2.0, ALU.mult, ALU.add))
            step(nc.vector.reciprocal(share[:, 0, :], share[:, 0, :]))
            step(nc.vector.tensor_tensor(share[:, 1, :], share[:, 1, :], share[:, 0, :], ALU.mult))

            def activate(t, u):
                dve.wait_ge(s_tanh_h, t + 1)
                after(dve, s_h_turned, t - 1)
                nc.vector.scalar_tensor_tensor(tanh_h[:, u % 2, :], tanh_h[:, u % 2, :], 1.0, bank_h[:, u % 2, 0, :],
                                               ALU.add, ALU.mult).then_inc(s_silu, 1)
                dve.wait_ge(s_silu, t + 1)
                nc.vector.tensor_tensor(act_h[:, u % 2, :], tanh_h[:, u % 2, :], bank_h[:, u % 2, 1, :], ALU.mult
                                        ).then_inc(s_act_h, 1)

            for u in range(MOE_BODY):
                activate(u, u)
            with dve.Fori(1, ROW_TILES // MOE_BODY) as i:
                for u in range(MOE_BODY):
                    activate(i * MOE_BODY + u, u)

            dve.wait_ge(s_tokens, 16 * B)
            for b in range(B):
                n, turn_no = b % 2, b // 2
                after(dve, s_out[n], 16 * turn_no)
                dve.wait_ge(s_gathered[n], 16 * 2 * TILES * (turn_no + 1))
                for r in range(2):
                    for t in range(TILES):
                        if r:
                            dve.wait_ge(s_mixed, 2 * TILES * b + t + 1)
                        nc.vector.scalar_tensor_tensor(
                            final[:, n, t, :], gathered[:, n, t, r, :], share[:, r, b * TILES + t:b * TILES + t + 1],
                            final[:, n, t, :] if r else tokens[:, b * TILES + t, :], ALU.mult, ALU.add
                        ).then_inc(s_mixed, 1)
                dve.wait_ge(s_mixed, 2 * TILES * (b + 1))
                layer_norm(final[:, n], s_ln4, s_rstd4, s_final, b)

        @block.gpsimd
        def _(pool):
            nc.gpsimd.memset(minus_half[:], -0.5).then_inc(s_prep, 1)
            nc.gpsimd.memset(rms_eps[:], HID * RMS_EPS).then_inc(s_prep, 1)
            pool.wait_ge(s_prep, PREPARED)

            def layer0(u, i):
                if 5 <= u < 5 + STATES:
                    n = u - 5
                    if n:
                        pool.wait_ge(l0.free_sem(f"C{n}"), l0.full_at(f"C{n}", i))
                    if n == 1 and not first(i):
                        pool.wait_ge(l0.full_sem("mix"), l0.full_at("mix", i - 1))
                    if n == 1:
                        nc.gpsimd.tensor_tensor(y[:], ch[:, 0, :, :], ch[:, 1, :, :], ALU.add).then_inc(s_ysum, 1)
                    if n > 1:
                        pool.wait_ge(s_ysum, at(i, STATES - 1, n - 1))
                        nc.gpsimd.tensor_tensor(y[:], y[:], ch[:, n % 2, :, :], ALU.add).then_inc(s_ysum, 1)
                if u == 14:
                    scale_of(s_ln0, s_rstd0, i)
                if u == 15:
                    scale_of(s_ln1, s_rstd1, i)

            def scale_of(step, scale, it):
                pool.wait_ge(step, at(it, LN_STEPS, LN_STEPS))
                nc.gpsimd.tensor_tensor(rstd[:], var[:], minus_half[:], ALU.pow).then_inc(scale, 1)

            def rms_of(c, j):
                pool.wait_ge(s_rms, at(j, TILES, c + 1))
                nc.gpsimd.tensor_tensor(rms[:, c:c + 1], rms[:, c:c + 1], rms_eps[:], ALU.add
                                        ).then_inc(s_rms_eps, 1)
                pool.wait_ge(s_rms_eps, at(j, TILES, c + 1))
                nc.gpsimd.tensor_tensor(rms[:, c:c + 1], rms[:, c:c + 1], minus_half[:, 0:1], ALU.pow
                                        ).then_inc(s_rms_pow, 1)

            def closing(j):
                rms_of(TILES - 1, j)
                scale_of(s_ln3, s_rstd3, j)

            def half_chunk(u, j):
                c, f = divmod(u - PAIRS, 2)
                if f == 0:
                    drained(pool, l1, j, f"e0_{c}", f"e1_{c}", *(f"q{p}" for p in range(PAIRS) if c == 0))
                    after(pool, s_O, at(j, 4 * TILES, 4 * c))
                    nc.gpsimd.tensor_tensor(qd[:], q[:, :, c * P:(c + 1) * P], from_start[:], ALU.mult
                                            ).then_inc(s_qd, 1)
                    if c:
                        rms_of(c - 1, j)

            def body(i, j):
                for u in range(UNITS):
                    if j is not None and u >= PAIRS:
                        half_chunk(u, j)
                    if i is not None:
                        layer0(u, i)
                if j is not None:
                    closing(j)

            rounds(pool, body)

            pool.wait_ge(s_rows_known, 1)
            pool.wait_ge(s_tokens, 16 * B)
            for t in range(TOK_TILES):
                for n in range(2):
                    nc.gpsimd.indirect_dma_start(
                        out=rows_dram, out_offset=bass.IndirectOffsetOnAxis(ap=row_of[:, n, t:t + 1], axis=0),
                        in_=tokens[:, t, :], in_offset=None).then_inc(s_scattered, 16)
            for n in range(2):
                pool.wait_ge(s_results[n], 16 * (ROW_TILES // MOE_BODY))
            for b in range(B):
                n, turn_no = b % 2, b // 2
                if b >= 2:
                    pool.wait_ge(s_mixed, 2 * TILES * (b - 1))
                for t in range(TILES):
                    for r in range(2):
                        nc.gpsimd.indirect_dma_start(
                            out=gathered[:, n, t, r, :], out_offset=None, in_=results_dram,
                            in_offset=bass.IndirectOffsetOnAxis(ap=row_of[:, r, b * TILES + t:b * TILES + t + 1], axis=0)
                        ).then_inc(s_gathered[n], 16)
                if b:
                    scale_of(s_ln4, s_rstd4, b - 1)
            scale_of(s_ln4, s_rstd4, B - 1)


def kernel(**inputs):
    import ml_dtypes
    import concourse.bacc as bacc
    from concourse.bass_utils import run_bass_kernel_spmd

    g = {n: np.ascontiguousarray(v) for n, v in inputs.items()}
    c = shape_constants()
    bf = ml_dtypes.bfloat16

    def rows(w):
        return w.reshape(-1, P, w.shape[1]).transpose(1, 0, 2)

    def thrice(w):
        full = np.zeros((w.shape[0], ROWS), w.dtype)
        for at_col in (0, PART2, PART3):
            full[:, at_col:at_col + w.shape[1]] = w
        return full

    w_in = g["L0_attn_W_in"]
    w_x = thrice(g["L0_attn_W_x"][:, STATES:])
    w_x[:, DT_ROW:DT_ROW + STATES] = g["L0_attn_W_x"][:, :STATES]
    arrays = {
        "x": g["L0_attn_x"],
        "eye": c["eye"], "from_last": c["from_last"], "eye_bf": c["eye"].astype(bf),
        "sel": c["sel"].astype(bf), "nsel": c["nsel"].astype(bf), "nselpair": c["nselpair"].astype(bf),
        "future": c["future"].astype(bf),
        "w_inT": rows(w_in[:, :2 * P].T), "taps": rows(g["L0_attn_dw_kernel"].T), "pw": rows(g["L0_attn_pw_kernel"]),
        "w_z": w_in[:, 2 * P:], "w_x": rows(w_x), "w_dt": g["L0_attn_W_dt"],
        "b_conv": g["L0_attn_conv_bias"].reshape(HALVES, P).T, "b_dt": g["L0_attn_b_dt"].reshape(HALVES, P).T,
        "d_skip": g["L0_attn_D"].reshape(HALVES, P).T, "a_log": rows(g["L0_attn_A_log"]),
        "w_out": rows(g["L0_attn_W_out"]), "w_ffn": g["L0_ffn_weight"].T,
        "w_q": g["L1_attn_Wq"].T, "w_k": g["L1_attn_Wk"].T, "w_v": g["L1_attn_Wv"].T,
        "w_g": g["L1_attn_Wg"].T, "w_og": g["L1_attn_Wog"].T, "w_o": rows(g["L1_attn_Wo"].T),
        "norm_w": g["L1_attn_norm_w"].reshape(PAIRS, P).T, "w_d": thrice(g["L1_attn_Wd"].T),
        "earlier": c["earlier"].astype(bf), "ones_bf": np.ones((P, P), bf), "rev": c["rev"],
        "tile_no": np.arange(moe_tiles(g["L0_attn_x"].shape[0] * T), dtype=np.float32)[None, :],
        "w_0": g["L1_ffn_w0"].transpose(1, 0, 2).reshape(P, EXPERTS * FF),
        "w_1": g["L1_ffn_w1"].transpose(1, 0, 2).reshape(P, EXPERTS * FF),
        "w_2": g["L1_ffn_wo"].reshape(EXPERTS, FCHUNKS, P, P).transpose(2, 0, 1, 3).reshape(P, EXPERTS * FF),
        "b_d": thrice(g["L1_attn_bd"][None, :]).T, "w_route": g["L1_ffn_gate_kernel"],
    }
    arrays = {n: np.ascontiguousarray(v) for n, v in arrays.items()}
    nc = bacc.Bacc("TRN2", target_bir_lowering=False, num_devices=1)
    aps = {n: nc.dram_tensor(n + "_dram", v.shape, mybir.dt.from_np(v.dtype), kind="ExternalInput").ap()
           for n, v in arrays.items()}
    out = nc.dram_tensor("out_dram", g["L0_attn_x"].shape, F32, kind="ExternalOutput").ap()
    build(nc, aps, out)
    r = run_bass_kernel_spmd(nc, [{n + "_dram": v for n, v in arrays.items()}], core_ids=[0])
    return r.results[0]["out_dram"]
```

```python
from contextlib import ExitStack

import numpy as np

import concourse.bass as bass
from concourse import mybir

P = 128
T = 512
TILES = T // P
HALVES = 2
STATES = 8
TAPS = 4
HEADS = 16
DH = 64
PAIRS = HEADS // 2
HID = HEADS * DH
EXPERTS = 8
FF = 512
FCHUNKS = FF // P
PART2, PART3, DT_ROW, ROWS = 64, 96, 32, 112

F32 = mybir.dt.float32
BF16 = mybir.dt.bfloat16
I32 = mybir.dt.int32
ALU = mybir.AluOpType
ACT = mybir.ActivationFunctionType
AX = mybir.AxisListType
LN_EPS = 1e-5
LN_STEPS = 11
RMS_EPS = float(np.finfo(np.float32).eps)


def head_of(g, h):
    return 8 * (g // 2) + g % 2 + 2 * h


def of_group(g):
    return slice(head_of(g, 0), head_of(g, 3) + 1, 2)


def shape_constants():
    part_rows = (0, PART2, PART3)
    sel = np.zeros((ROWS, HEADS, P), np.float32)
    selpair = np.zeros((ROWS, PAIRS, P), np.float32)
    for r in part_rows:
        for h in range(HEADS):
            sel[r + h, h, :] = 1.0
            selpair[r + h, h // 2, (h % 2) * DH:(h % 2 + 1) * DH] = 1.0
    j, i = np.mgrid[0:P, 0:P]
    future = np.where(i < j, -1e30, 0.0).astype(np.float32)
    eye = np.eye(P, dtype=np.float32)
    from_last = eye - (j == P - 1)
    earlier = (j < i).astype(np.float32)
    return {
        "sel": sel, "nsel": -sel, "nselpair": -selpair, "future": np.tile(future, (1, 4)),
        "rev": np.tile(EXPERTS - np.arange(EXPERTS, dtype=np.float32), (P, 1)),
        "eye": eye, "from_last": from_last.astype(np.float32), "earlier": earlier,
    }


def at(it, per_round, k):
    return it * per_round + k


def after(eng, sem, value):
    if isinstance(value, int) and value <= 0:
        return
    eng.wait_ge(sem, value)


def first(it):
    return isinstance(it, int) and it == 0


def moe_tiles(tokens):
    worst = 2 * tokens // P + EXPERTS
    return -(-worst // MOE_BODY) * MOE_BODY


END = "end"


def state_within(u, i, j):
    step = L0_STEPS[u][0] if L0_STEPS[u] else 0
    return step - 5 if i is not None and j is not None and u >= PAIRS and 5 <= step < 5 + STATES else None


class Ring:

    def __init__(self, banks, filled, drained, uses, late=(), rounds=0):
        self.banks, self.filled, self.drained = banks, filled, drained
        self.n = len(filled)
        self.rounds = rounds
        self.place = {}
        self.early = {}
        self.last = {}
        self.per = [0] * self.n
        self.late = [0] * self.n
        for k, use in enumerate(uses):
            b = k % self.n
            self.per[b] += 1
            self.place[use] = (b, self.per[b])
            if use in late:
                self.late[b] += 1
                self.last[use] = self.late[b]
            else:
                self.early[use] = self.per[b] - self.late[b]

    def bank(self, use):
        return self.banks[:, self.place[use][0], :]

    def free_sem(self, use):
        return self.drained[self.place[use][0]]

    def full_sem(self, use):
        return self.filled[self.place[use][0]]

    def full_at(self, use, it):
        b, k = self.place[use]
        if it is END:
            return at(self.rounds, self.per[b], self.last[use] - self.late[b])
        if first(it):
            return self.early[use]
        return at(it, self.per[b], k - self.late[b])

    def free_at(self, use, it):
        return self.full_at(use, it) - 1


L0_USES = (["xT", "u0", "u1", "xdbl", "dt0", "dt1", "z0", "z1"]
           + [f"{c}{n}" for n in range(STATES) for c in "BC"] + ["mix", "x1T", "ffn"])


def l1_uses():
    uses = ["x2T"] + L1_LATE[-1] + ["wd"]
    for u in range(PAIRS):
        uses += [f"q{u}", f"g{u}"]
        uses += ["cpT"] if u == 6 else ["cpd"] if u == 7 else []
        uses += L1_LATE[u] if u in L1_LATE else []
    for c in range(TILES):
        uses += [f"v0_{c}", f"v1_{c}", f"o0_{c}", f"o1_{c}", f"e0_{c}", f"e1_{c}", f"kT0_{c}", f"kT1_{c}",
                 f"D0_{c}", f"S0_{c}"]
        uses += [f"OT0_{c - 1}", f"OT1_{c - 1}"] if c else []
        uses += [f"D1_{c}", f"S1_{c}"]
        uses += [f"wo_{c - 1}"] if c else []
        uses += [f"D2_{c}", f"S2_{c}", f"D3_{c}", f"S3_{c}"]
        uses += [f"U_{c}"] if c < TILES - 1 else []
    return uses


L1_LATE = {-1: [f"OT0_{TILES - 1}", f"OT1_{TILES - 1}"], 0: [f"wo_{TILES - 1}"], 4: ["x3T"], 5: ["route"]}


MOE_BODY = 8
ZERO_ROWS = 8
MOE_LOAD = 4
UNITS = 16

L0_STEPS = [[3], [4], [], [2], [5], [], [6], [7], [8], [9], [10], [11], [12, 13], [14], [15], []]
LOGS = 2
Q_BY_DVE = (2, 3)

def build(nc, a, out):
    B = a["x"].shape[0]
    TOK_TILES = B * TILES
    ROW_TILES = moe_tiles(B * T)
    with ExitStack() as ctx:
        attention = ExitStack()

        def sb(name, shape, dt=F32):
            return attention.enter_context(nc.sbuf_tensor(name, shape, dt))

        def sb_kept(name, shape, dt=F32):
            return ctx.enter_context(nc.sbuf_tensor(name, shape, dt))

        logits = sb_kept("logits", [P, TOK_TILES, EXPERTS])
        eye = sb_kept("eye", [P, P])
        minus_half = sb_kept("minus_half", [P, TILES])
        rms_eps = sb_kept("rms_eps", [P, 1])
        earlier = sb_kept("earlier", [P, P], BF16)
        ones_bf = sb_kept("ones_bf", [P, P], BF16)
        rev = sb_kept("rev", [P, EXPERTS])
        tile_no = sb_kept("tile_no", [1, ROW_TILES])
        stats = sb_kept("stats", [P, TILES, 6])
        mean = sb_kept("mean", [P, TILES])
        apart = sb_kept("apart", [P, TILES])
        var = sb_kept("var", [P, TILES])
        rstd = sb_kept("rstd", [P, TILES])

        def sem(name):
            return ctx.enter_context(nc.semaphore(name))

        eye_bf = sb("eye_bf", [P, P], BF16)
        sel = sb("sel", [ROWS, HEADS, P], BF16)
        nsel = sb("nsel", [ROWS, HEADS, P], BF16)
        nselpair = sb("nselpair", [ROWS, PAIRS, P], BF16)
        future = sb("future", [P, 4 * P], BF16)
        from_last = sb("from_last", [P, P])
        taps = sb("taps", [P, HALVES, TAPS])
        w_conv = sb("w_conv", [P, TAPS, 2 * P])
        w_z = sb("w_z", [P, 2 * P])
        w_x = sb("w_x", [P, HALVES, ROWS])
        w_dt = sb("w_dt", [P, 2 * P])
        b_conv = sb("b_conv", [P, HALVES])
        b_dt = sb("b_dt", [P, HALVES])
        d_skip = sb("d_skip", [P, HALVES])
        a_neg = sb("a_neg", [P, HALVES, STATES])
        a_log = sb("a_log", [P, HALVES, STATES])
        w_out = sb("w_out", [P, HALVES, P])
        w_ffn = sb("w_ffn", [P, P])
        w_sign = sb("w_sign", [P, P])
        w_less = sb("w_less", [P, P])
        w_q = sb("w_q", [P, HID])
        w_k = sb("w_k", [P, HID])
        w_v = sb("w_v", [P, HID])
        w_g = sb("w_g", [P, HID])
        w_og = sb("w_og", [P, HID])
        w_o = sb("w_o", [P, PAIRS, P])
        norm_w = sb("norm_w", [P, PAIRS])
        w_d = sb("w_d", [P, ROWS])
        b_d = sb("b_d", [ROWS, 1])
        w_route = sb("w_route", [P, EXPERTS])
        ones = sb("ones", [ROWS, P])

        x_tok = sb("x_tok", [P, TILES, P])
        xT = sb("xT", [P, TAPS - 1 + T])
        xc = sb("xc", [P, HALVES, T])
        th = sb("th", [P, HALVES, T])
        sz = sb("sz", [P, HALVES, T])
        parts = sb("parts", [ROWS, T], BF16)
        rest = sb("rest", [ROWS, T])
        dt_raw = sb("dt_raw", [P, T])
        delta = sb("delta", [P, HALVES, T])
        du = sb("du", [P, HALVES, T])
        decay = sb("decay", [P, 2, HALVES, T])
        push = sb("push", [P, HALVES, T])
        hs = sb("hs", [P, HALVES, T])
        ch = sb("ch", [P, 2, HALVES, T])
        y = sb("y", [P, HALVES, T])
        x1 = sb("x1", [P, TILES, P])
        x1T = sb("x1T", [P, T])
        x2_new = sb("x2_new", [P, TILES, P])

        x3 = sb("x3", [P, TILES, P])
        x2T = sb("x2T", [P, T])
        sp_in = sb("sp_in", [ROWS, T])
        sp_ln = sb("sp_ln", [ROWS, T])
        fall = sb("fall", [ROWS, T])
        fall_parts = sb("fall_parts", [ROWS, T], BF16)
        fall_rest = sb("fall_rest", [ROWS, T])
        fall_tok = sb("fall_tok", [P, TILES * HEADS])
        to_end = sb("to_end", [P, TILES, HEADS])
        q = sb("q", [P, PAIRS, T])
        k = sb("k", [P, PAIRS, T])
        tg = sb("tg", [P, 2, T])
        v = sb("v", [P, HID])
        tog = sb("tog", [P, HID])
        from_start = sb("from_start", [P, PAIRS, P])
        qd = sb("qd", [P, PAIRS, P])
        kd = sb("kd", [P, HEADS, DH])
        E = sb("E", [P, 2, 4 * P])
        pw = E[:, 0, :].rearrange("p (c n) -> p c n", c=HALVES)
        w_inT = E[:, 1, 0:2 * P].rearrange("p (c n) -> p c n", c=HALVES)
        w_tap = E[:, 1, 2 * P:4 * P].rearrange("p (c n) -> p c n", c=HALVES)
        S = sb("S", [P, 2, 4 * P])
        state = sb("state", [P, PAIRS, 2 * DH])
        o = sb("o", [P, HID])
        oT = sb("oT", [P, PAIRS, P])
        sq = sb("sq", [P, T], BF16)
        ssq = sb("ssq", [P, TILES, 2])
        rms = sb("rms", [P, TILES])
        x3T = sb("x3T", [P, T])
        zeros = q[:, 0:2, :].rearrange("p a n -> p (a n)")
        attention.close()

        w_0 = sb_kept("w_0", [P, EXPERTS * FF])
        w_1 = sb_kept("w_1", [P, EXPERTS * FF])
        w_2 = sb_kept("w_2", [P, EXPERTS * FF])
        tokens = sb_kept("tokens", [P, TOK_TILES, P])
        best = sb_kept("best", [P, 2, TOK_TILES])
        place = sb_kept("place", [P, 2, TOK_TILES])
        hot = sb_kept("hot", [P, 2, TOK_TILES, EXPERTS])
        hot_bf = sb_kept("hot_bf", [P, TOK_TILES, EXPERTS], BF16)
        work = sb_kept("work", [P, TOK_TILES, EXPERTS])
        rank = sb_kept("rank", [P, TOK_TILES, EXPERTS])
        total = sb_kept("total", [P, EXPERTS, TOK_TILES])
        upto = sb_kept("upto", [P, EXPERTS, TOK_TILES])
        ones_r = sb_kept("ones_r", [P, TOK_TILES])
        count_i = sb_kept("count_i", [P, EXPERTS], I32)
        tiles_of = sb_kept("tiles_of", [P, EXPERTS])
        ends = sb_kept("ends", [P, EXPERTS])
        base = sb_kept("base", [P, EXPERTS])
        share = sb_kept("share", [P, 2, TOK_TILES])
        row_of = sb_kept("row_of", [P, 2, TOK_TILES], I32)
        past = sb_kept("past", [1, ROW_TILES, EXPERTS])
        expert_f = sb_kept("expert_f", [1, ROW_TILES])
        expert_i = sb_kept("expert_i", [1, ROW_TILES], I32)
        rows_in = sb_kept("rows_in", [P, 2, MOE_LOAD, P])
        rowsT = sb_kept("rowsT", [P, 2, MOE_LOAD * P])
        tanh_h = sb_kept("tanh_h", [P, 2, FF])
        act_h = sb_kept("act_h", [P, 4, FF])
        w_here = sb_kept("w_here", [P, 2, 2, FF])
        rows_out = sb_kept("rows_out", [P, 2, MOE_LOAD, P])
        gathered = sb_kept("gathered", [P, 2, TILES, 2, P])
        final = sb_kept("final", [P, 2, TILES, P])

        x3_dram = nc.dram_tensor("x3_scratch", [B, T, P], F32, kind="Internal").ap().rearrange(
            "b (c p) d -> b p c d", p=P)
        rows_dram = nc.dram_tensor("rows_scratch", [ROW_TILES * P, P], F32, kind="Internal").ap()
        results_dram = nc.dram_tensor("results_scratch", [ROW_TILES * P, P], F32, kind="Internal").ap()

        banks = ctx.enter_context(nc.psum_tensor("banks", [P, 8, T], F32))
        l0_banks, l1_banks, o_banks = banks[:, 0:3, :], banks[:, 3:6, :], banks[:, 6:8, :]
        bank_h = banks[:, 0:4, :].rearrange("p (u m) f -> p u m f", u=2)
        bank_y, bank_rows = banks[:, 4:6, :], banks[:, 6:8, :]

        s_weights = sem("weights_loaded")
        s_wtap = sem("w_tap_ready")
        s_wmul = sem("w_conv_multiplied")
        s_wconv = sem("w_conv_copied")
        s_prep = sem("weights_prepared")
        s_alog = sem("a_log_exp")
        s_sign = sem("sign_steps")
        l0 = Ring(l0_banks, [sem(f"l0_filled{b}") for b in range(3)],
                  [sem(f"l0_drained{b}") for b in range(3)], L0_USES)
        l1 = Ring(l1_banks, [sem(f"l1_filled{b}") for b in range(3)],
                  [sem(f"l1_drained{b}") for b in range(3)], l1_uses(),
                  late=sum(L1_LATE.values(), []), rounds=B)
        lk = Ring(o_banks, [sem(f"key_filled{b}") for b in range(2)],
                  [sem(f"key_drained{b}") for b in range(2)], [f"k{u}" for u in range(PAIRS)])
        s_x_loaded = sem("x_loaded")
        s_hu = sem("half_u_ready")
        s_tanh = sem("tanh_ready")
        s_xc = sem("xc_ready")
        s_dt_raw = sem("dt_raw_ready")
        s_split = sem("split_steps")
        s_dtb = sem("dt_biased")
        s_sp = sem("softplus_steps")
        s_delta = sem("delta_ready")
        s_du = sem("du_ready")
        s_decay = sem("decay_ready")
        s_push = sem("push_ready")
        s_scan = sem("scan_ready")
        s_ch = sem("ch_ready")
        s_ysum = sem("y_summed")
        s_ygate = sem("y_gate_steps")
        s_y = sem("y_ready")
        s_ln0 = sem("ln0_steps")
        s_ln1 = sem("ln1_steps")
        s_x1 = sem("x1_ready")
        s_x1T = sem("x1T_ready")
        s_x2 = sem("x2_ready")
        s_x2_taken = sem("x2_taken")

        s_x2T = sem("x2T_ready")
        s_dsp = sem("decay_softplus_act")
        s_dlog = sem("decay_softplus_ready")
        s_fall = sem("fall_ready")
        s_fsplit = sem("fall_split_steps")
        s_ftok = sem("fall_tok_ready")
        s_toend = sem("to_end_ready")
        s_q = sem("q_ready")
        s_tg = sem("gate_tanh_ready")
        s_k = sem("k_ready")
        s_v = sem("v_ready")
        s_tog = sem("out_gate_tanh_ready")
        s_fs = sem("from_start_ready")
        s_qd = sem("q_decayed")
        s_kd = sem("k_decayed")
        s_E = sem("mask_ready")
        s_S = sem("scores_ready")
        s_O = sem("o_filled")
        s_osq = sem("o_squared")
        s_og = sem("o_gated")
        s_half_state = sem("state_first_half")
        s_decst = sem("state_decayed")
        s_state = sem("state_ready")
        s_oT = sem("oT_ready")
        s_rms = sem("rms_steps")
        s_rms_pow = sem("rms_ready")
        s_ln3 = sem("ln3_steps")
        s_rstd0 = sem("ln0_scale")
        s_rms_eps = sem("rms_eps_added")
        s_rstd1 = sem("ln1_scale")
        s_rstd3 = sem("ln3_scale")
        s_x3 = sem("x3_ready")
        s_x3T = sem("x3T_ready")
        s_x3_stored = sem("x3_stored")
        s_cleared = sem("rows_cleared")
        s_zero = sem("zeros_ready")
        s_w_moe = sem("expert_weights_loaded")
        s_tokens = sem("tokens_loaded")
        s_route = sem("route_steps")
        s_counted = sem("ranks_counted")
        s_share = sem("share_exp")
        s_rows_known = sem("row_of_ready")
        s_expert = sem("expert_ready")
        s_scattered = sem("rows_scattered")
        s_rows_in = [sem("rows_in_loaded0"), sem("rows_in_loaded1")]
        s_turned = sem("rows_turned")
        s_rowsT = sem("rowsT_ready")
        s_h = sem("h_multiplied")
        s_tanh_h = sem("tanh_h_ready")
        s_silu = sem("silu_ready")
        s_act_h = sem("act_h_ready")
        s_w_here = sem("w_here_ready")
        s_y_tile = sem("result_multiplied")
        s_rows_out = sem("result_copied")
        s_results = [sem("results_stored0"), sem("results_stored1")]
        s_gathered = [sem("results_gathered0"), sem("results_gathered1")]
        s_mixed = sem("results_mixed")
        s_ln4 = sem("ln4_steps")
        s_rstd4 = sem("ln4_scale")
        s_final = sem("final_ready")
        s_out = [sem("out_stored0"), sem("out_stored1")]

        loads = [
            (eye[:], a["eye"]), (eye_bf[:], a["eye_bf"]), (sel[:], a["sel"]), (nsel[:], a["nsel"]),
            (nselpair[:], a["nselpair"]), (future[:], a["future"]), (from_last[:], a["from_last"]),
            (w_inT[:], a["w_inT"]), (taps[:], a["taps"]), (pw[:], a["pw"]), (w_z[:], a["w_z"]), (w_x[:], a["w_x"]),
            (w_dt[DT_ROW:DT_ROW + 8, :], a["w_dt"]), (b_conv[:], a["b_conv"]), (b_dt[:], a["b_dt"]),
            (d_skip[:], a["d_skip"]), (a_log[:], a["a_log"]), (w_out[:], a["w_out"]), (w_ffn[:], a["w_ffn"]),
            (w_q[:], a["w_q"]), (w_k[:], a["w_k"]), (w_v[:], a["w_v"]), (w_g[:], a["w_g"]), (w_og[:], a["w_og"]),
            (w_o[:], a["w_o"]), (norm_w[:], a["norm_w"]), (w_d[:], a["w_d"]), (b_d[:], a["b_d"]),
            (w_route[:], a["w_route"]), (earlier[:], a["earlier"]), (ones_bf[:], a["ones_bf"]), (rev[:], a["rev"]),
            (tile_no[:], a["tile_no"]),
        ]
        WEIGHTS = 16 * len(loads)
        PREPARED = 10 + PAIRS
        x_dram = a["x"].rearrange("b (c p) d -> b p c d", p=P)
        out_dram = out.rearrange("b (c p) d -> b p c d", p=P)
        zero_dram = rows_dram.rearrange("(n p r) d -> n p (r d)", p=P, r=ZERO_ROWS)
        rows_in_dram = rows_dram.rearrange("(n c p) d -> n p c d", c=MOE_LOAD, p=P)
        rows_out_dram = results_dram.rearrange("(n c p) d -> n p c d", c=MOE_LOAD, p=P)

        def drained(eng, ring, it, *uses):
            last = {}
            for use in uses:
                bank, count = ring.place[use]
                if bank not in last or count > ring.place[last[bank]][1]:
                    last[bank] = use
            for use in last.values():
                eng.wait_ge(ring.free_sem(use), ring.full_at(use, it))

        ROUTE_HOT = 12
        ROUTE_BEST = ROUTE_HOT + 1
        ROUTE_TAKEN = ROUTE_BEST + 3

        block = ctx.enter_context(nc.Block())

        def rounds(eng, body):
            body(0, None)
            body(1, 0)
            with eng.Fori(2, B) as r:
                body(r, r - 1)
            body(None, B - 1)

        def attention_over(eng):
            drained(eng, l1, END, "route")
            eng.wait_ge(s_x3, B * TILES)

        @block.sync
        def _(sp):
            for dst, src in loads:
                sp.dma_start(dst, src).then_inc(s_weights, 16)

            def body(i, j):
                if i is not None:
                    if not first(i):
                        drained(sp, l0, i - 1, "mix")
                    sp.dma_start(x_tok[:], x_dram[bass.ds(i, 1)].rearrange("b p c d -> (b p) c d")
                                 ).then_inc(s_x_loaded, 16)
                if j is not None and not first(j):
                    store_x3(j - 1)

            def store_x3(j):
                sp.wait_ge(s_x3, at(j, TILES, TILES))
                sp.dma_start(x3_dram[bass.ds(j, 1)].rearrange("b p c d -> (b p) c d"), x3[:]
                             ).then_inc(s_x3_stored, 16)

            sp.wait_ge(s_zero, 1)
            for n in range(ROW_TILES // ZERO_ROWS):
                sp.dma_start(zero_dram[n], zeros).then_inc(s_cleared, 16)
            rounds(sp, body)
            store_x3(B - 1)

            attention_over(sp)
            sp.wait_ge(s_x3_stored, 16 * B)
            for b in range(B):
                sp.dma_start(tokens[:, b * TILES:(b + 1) * TILES, :], x3_dram[b]).then_inc(s_tokens, 16)
            for dst, name in ((w_0, "w_0"), (w_1, "w_1"), (w_2, "w_2")):
                sp.dma_start(dst[:], a[name]).then_inc(s_w_moe, 16)
            sp.wait_ge(s_scattered, 16 * 2 * TOK_TILES)

            def load_rows(i):
                for n in range(2):
                    g = 2 * i + n
                    if not first(i):
                        sp.wait_ge(s_turned, g - 1)
                    sp.dma_start(rows_in[:, n], rows_in_dram[bass.ds(g, 1)].rearrange("n p c d -> (n p) c d")
                                 ).then_inc(s_rows_in[n], 16)

            def store_results(i):
                for n in range(2):
                    g = 2 * i + n
                    sp.wait_ge(s_rows_out, MOE_LOAD * (g + 1))
                    sp.dma_start(rows_out_dram[bass.ds(g, 1)].rearrange("n p c d -> (n p) c d"), rows_out[:, n]
                                 ).then_inc(s_results[n], 16)

            load_rows(0)
            with sp.Fori(0, ROW_TILES // MOE_BODY - 1) as i:
                load_rows(i + 1)
                store_results(i)
            store_results(ROW_TILES // MOE_BODY - 1)

            def store(b, n):
                sp.wait_ge(s_final, TILES * (b + 1))
                sp.dma_start(out_dram[bass.ds(b, 1)].rearrange("b p c d -> (b p) c d"), final[:, n]
                             ).then_inc(s_out[n], 16)

            for b in range(B):
                store(b, b % 2)
            for n in range(2):
                sp.wait_ge(s_out[n], 16 * ((B + 1 - n) // 2))

        @block.tensor
        def _(pe):
            pe.wait_ge(s_weights, WEIGHTS)
            for t in range(TAPS):
                pe.wait_ge(s_wtap, HALVES * (t + 1))
                if t >= 1:
                    pe.wait_ge(s_wconv, t)
                for c in range(HALVES):
                    mm = pe.matmul(l0_banks[:, 0, 0:2 * P], w_tap[:, c, :], pw[:, c, :],
                                   start=(c == 0), stop=(c == 1))
                mm.then_inc(s_wmul, 1)
            pe.wait_ge(s_wconv, TAPS)
            pe.wait_ge(s_prep, PREPARED)

            def fill(ring, use, it, *needs):
                drained(pe, ring, it, *(n for n in needs if ring.place[n][0] != ring.place[use][0]))
                after(pe, ring.free_sem(use), ring.free_at(use, it))
                return ring.bank(use), ring.full_sem(use)

            def turn(ring, use, src, it):
                bank, full = fill(ring, use, it)
                for t in range(TILES):
                    mm = pe.transpose(bank[:, t * P:(t + 1) * P], src[:, t, :], eye[:])
                mm.then_inc(full, 1)

            def layer0(u, i):
                if u == 0:
                    pe.wait_ge(s_x_loaded, at(i, 16, 16))
                    turn(l0, "xT", x_tok, i)
                if u == 1:
                    for h in range(HALVES):
                        bank, full = fill(l0, f"u{h}", i, "xT")
                        for t in range(TAPS):
                            mm = pe.matmul(bank, w_conv[:, t, h * P:(h + 1) * P], xT[:, t:t + T],
                                           start=(t == 0), stop=(t == TAPS - 1))
                        mm.then_inc(full, 1)
                if u == 2:
                    for h in range(HALVES):
                        bank, full = fill(l0, f"z{h}", i)
                        pe.matmul(bank, w_z[:, h * P:(h + 1) * P], xT[:, TAPS - 1:TAPS - 1 + T],
                                  start=True, stop=True).then_inc(full, 1)
                if u == 3:
                    pe.wait_ge(s_xc, at(i, HALVES, HALVES))
                    bank, full = fill(l0, "xdbl", i)
                    for h in range(HALVES):
                        mm = pe.matmul(bank[0:ROWS, :], w_x[:, h, :], xc[:, h, :], start=(h == 0), stop=(h == 1))
                    mm.then_inc(full, 1)
                if u == 4:
                    pe.wait_ge(s_dt_raw, at(i, 1, 1))
                    for h in range(HALVES):
                        bank, full = fill(l0, f"dt{h}", i)
                        pe.matmul(bank, w_dt[DT_ROW:DT_ROW + 8, h * P:(h + 1) * P],
                                  dt_raw[DT_ROW:DT_ROW + 8, :], start=True, stop=True).then_inc(full, 1)
                if 5 <= u < 5 + STATES:
                    n = u - 5
                    if n == 0:
                        pe.wait_ge(s_split, at(i, 4, 4))
                    for c, row in (("B", n), ("C", STATES + n)):
                        bank, full = fill(l0, f"{c}{n}", i)
                        pe.matmul(bank, sel[:, row, :], parts[:], start=True, stop=True).then_inc(full, 1)
                if u == 14:
                    pe.wait_ge(s_y, at(i, HALVES, HALVES))
                    bank, full = fill(l0, "mix", i)
                    for t in range(TILES):
                        for h in range(HALVES):
                            mm = pe.matmul(bank[:, t * P:(t + 1) * P], y[:, h, t * P:(t + 1) * P],
                                           w_out[:, h, :], start=(h == 0), stop=(h == 1))
                    mm.then_inc(full, 1)
                if u == 15:
                    pe.wait_ge(s_x1, at(i, TILES, TILES))
                    turn(l0, "x1T", x1, i)
                    bank, full = fill(l0, "ffn", i, "x1T")
                    for t in range(TILES):
                        mm = pe.matmul(bank[:, t * P:(t + 1) * P], x1T[:, t * P:(t + 1) * P], w_sign[:],
                                       start=True, stop=True)
                    mm.then_inc(full, 1)

            def opening(j):
                pe.wait_ge(s_x2, at(j, TILES, TILES))
                turn(l1, "x2T", x2_new, j)

            def log_decay(j):
                bank, full = fill(l1, "wd", j, "x2T")
                pe.matmul(bank[0:ROWS, :], w_d[:], x2T[:], start=True, stop=True).then_inc(full, 1)

            def project(u, j):
                for name, w in (("q", w_q), ("g", w_g), ("k", w_k)):
                    if name == "k" and u < 2:
                        after(pe, s_osq, at(j, 2 * TILES, u - 1))
                        after(pe, s_og, at(j, 2 * TILES, u - 1))
                    bank, full = fill(lk if name == "k" else l1, f"{name}{u}", j)
                    pe.matmul(bank, w[:, u * P:(u + 1) * P], x2T[:], start=True, stop=True).then_inc(full, 1)
                if u == 6:
                    pe.wait_ge(s_fall, at(j, TILES, TILES))
                    bank, full = fill(l1, "cpT", j)
                    for c in range(TILES):
                        mm = pe.transpose(bank[:, c * ROWS:(c + 1) * ROWS], fall[:, c * P:(c + 1) * P],
                                          eye[0:ROWS, 0:ROWS])
                    mm.then_inc(full, 1)
                if u == 7:
                    bank, full = fill(l1, "cpd", j, "cpT")
                    pe.matmul(bank[:, 0:TILES * HEADS], from_last[:], fall_tok[:], start=True, stop=True
                              ).then_inc(full, 1)

            def mask(g, c, j):
                bank, full = fill(l1, f"D{g}_{c}", j)
                here = slice(c * P, (c + 1) * P)
                pe.matmul(bank, fall_parts[:, here], sel[:, of_group(g), :], start=True, stop=False)
                pe.matmul(bank, eye_bf[:], future[:], start=False, stop=False)
                for h in range(4):
                    mm = pe.matmul(bank[:, h * P:(h + 1) * P], nsel[:, head_of(g, h), :], fall_parts[:, here],
                                   start=False, stop=(h == 3))
                mm.then_inc(full, 1)

            def scores(g, c, j):
                bank, full = fill(l1, f"S{g}_{c}", j)
                here = slice(c * P, (c + 1) * P)
                for h in range(4):
                    pair, rows = head_of(g, h) // 2, slice(g % 2 * DH, (g % 2 + 1) * DH)
                    mm = pe.matmul(bank[:, h * P:(h + 1) * P], k[rows, pair, here], q[rows, pair, here],
                                   start=True, stop=True)
                mm.then_inc(full, 1)

            def outputs(g, c, j):
                needs = [f"S{g}_{c}"]
                if g == 0:
                    needs += [f"v0_{c}", f"v1_{c}"] + ([f"U_{c - 1}"] if c else [])
                drained(pe, l1, j, *needs)
                if g % 2 == 0:
                    after(pe, s_osq, at(j, 2 * TILES, 2 * (c - 1) + g // 2 + 1))
                    after(pe, s_og, at(j, 2 * TILES, 2 * (c - 1) + g // 2 + 1))
                if g == 0:
                    pe.wait_ge(s_qd, at(j, TILES, c + 1))
                    if c:
                        pe.wait_ge(s_half_state, at(j, TILES - 1, c))
                for h in range(4):
                    head = head_of(g, h)
                    pair = head // 2
                    if c and g % 2 == 0:
                        pe.matmul(o_banks[:, g // 2, pair % 4 * P:(pair % 4 + 1) * P], qd[:, pair, :],
                                  state[:, pair, :], start=(h == 0), stop=False)
                    to = o_banks[:, g // 2, head % 8 * DH:(head % 8 + 1) * DH]
                    mm = pe.matmul(to, S[:, g % 2, h * P:(h + 1) * P], v[:, head * DH:(head + 1) * DH],
                                   start=(c == 0), stop=(c == 0 or (g % 2 == 1 and h == 3)))
                mm.then_inc(s_O, 1)

            def update(c, j):
                bank, full = fill(l1, f"U_{c}", j, f"kT0_{c}", f"kT1_{c}")
                for head in range(HEADS):
                    rows = slice(head % 2 * DH, (head % 2 + 1) * DH)
                    mm = pe.matmul(bank[rows, head // 2 * DH:(head // 2 + 1) * DH], kd[:, head, :],
                                   v[:, head * DH:(head + 1) * DH], start=True, stop=True)
                mm.then_inc(full, 1)

            def turn_out(c, j, it):
                for f in range(2):
                    pe.wait_ge(s_og, at(j, 2 * TILES, 2 * c + f + 1))
                    bank, full = fill(l1, f"OT{f}_{c}", it)
                    for t in range(4):
                        mm = pe.transpose(bank[:, t * P:(t + 1) * P], o[:, (4 * f + t) * P:(4 * f + t + 1) * P],
                                          eye[:])
                    mm.then_inc(full, 1)

            def project_out(c, it):
                bank, full = fill(l1, f"wo_{c}", it, f"OT0_{c}", f"OT1_{c}")
                for t in range(PAIRS):
                    mm = pe.matmul(bank[:, 0:P], oT[:, t, :], w_o[:, t, :], start=(t == 0), stop=(t == PAIRS - 1))
                mm.then_inc(full, 1)

            def half_chunk(u, i, j):
                c, f = divmod(u - PAIRS, 2)
                within = state_within(u, i, j)
                if f and within is not None:
                    layer0(5 + within, i)
                here = slice(c * P, (c + 1) * P)
                if f == 0:
                    for name, w in (("v", w_v), ("o", w_og)):
                        for n in range(2):
                            bank, full = fill(l1, f"{name}{n}_{c}", j)
                            pe.matmul(bank, x2T[:, here], w[:, n * T:(n + 1) * T], start=True, stop=True
                                      ).then_inc(full, 1)
                        if name == "v" and u == PAIRS and i is not None:
                            layer0(L0_STEPS[u - 1][0], i)
                        if name == "o" and within is not None:
                            layer0(5 + within, i)
                    if c == 0:
                        pe.wait_ge(s_fsplit, at(j, 5, 5))
                    for n in range(2):
                        queries = [f"q{p}" for p in range(PAIRS)] if c == 0 and n == 0 else []
                        bank, full = fill(l1, f"e{n}_{c}", j, *queries)
                        for t in range(4):
                            mm = pe.matmul(bank[:, t * P:(t + 1) * P], nselpair[:, 4 * n + t, :],
                                           fall_parts[:, here], start=True, stop=True)
                        mm.then_inc(full, 1)
                    for n in range(2):
                        if c == 0 and n == 0:
                            drained(pe, lk, j, *(f"k{p}" for p in range(PAIRS)))
                        bank, full = fill(l1, f"kT{n}_{c}", j)
                        for t in range(4):
                            mm = pe.transpose(bank[:, t * P:(t + 1) * P], k[:, 4 * n + t, here], eye[:])
                        mm.then_inc(full, 1)
                    mask(0, c, j)
                    scores(0, c, j)
                    if c:
                        turn_out(c - 1, j, j)
                    mask(1, c, j)
                    scores(1, c, j)
                    if c:
                        project_out(c - 1, j)
                    outputs(0, c, j)
                else:
                    mask(2, c, j)
                    scores(2, c, j)
                    outputs(1, c, j)
                    mask(3, c, j)
                    scores(3, c, j)
                    outputs(2, c, j)
                    outputs(3, c, j)
                    if c < TILES - 1:
                        update(c, j)

            def closing(u, j, it):
                if u == -1:
                    turn_out(TILES - 1, j, it)
                if u == 0:
                    project_out(TILES - 1, it)
                if u == 4:
                    pe.wait_ge(s_x3, at(j, TILES, TILES))
                    turn(l1, "x3T", x3, it)
                if u == 5:
                    bank, full = fill(l1, "route", it, "x3T")
                    for t in range(TILES):
                        mm = pe.matmul(bank[:, t * EXPERTS:(t + 1) * EXPERTS], x3T[:, t * P:(t + 1) * P], w_route[:],
                                       start=True, stop=True)
                    mm.then_inc(full, 1)

            def body(i, j):
                if j is not None:
                    opening(j)
                if i is not None:
                    layer0(0, i)
                if j is not None and not first(j):
                    closing(-1, j - 1, j)
                if j is not None:
                    log_decay(j)
                if i is not None:
                    layer0(1, i)
                for u in range(UNITS):
                    within = state_within(u, i, j)
                    if j is not None:
                        project(u, j) if u < PAIRS else half_chunk(u, i, j)
                        if u < PAIRS and not first(j):
                            closing(u, j - 1, j)
                    for n in L0_STEPS[u] if i is not None else ():
                        if (within is None or n != 5 + within) and (j is None or u != PAIRS - 1):
                            layer0(n, i)

            rounds(pe, body)
            for u in range(-1, PAIRS):
                closing(u, B - 1, END)

            pe.wait_ge(s_route, ROUTE_HOT)
            drained(pe, l1, END, "route")
            pe.matmul(l1_banks[:, 0, 0:TOK_TILES * EXPERTS], earlier[:], hot_bf[:], start=True, stop=True)
            pe.matmul(l1_banks[:, 1, 0:TOK_TILES * EXPERTS], ones_bf[:], hot_bf[:], start=True, stop=True
                      ).then_inc(s_counted, 1)

            def turn_rows(i, n):
                g = 2 * i + n
                pe.wait_ge(s_rows_in[n], at(i, 16, 16))
                after(pe, s_rowsT, g - 1 if n or not first(i) else 0)
                for t in range(MOE_LOAD):
                    mm = pe.transpose(bank_rows[:, n, t * P:(t + 1) * P], rows_in[:, n, t, :], eye[:])
                mm.then_inc(s_turned, 1)

            def hidden(t, u):
                if u % MOE_LOAD == 0:
                    pe.wait_ge(s_rowsT, t // MOE_LOAD + 1 if isinstance(t, int) else (t - u) // MOE_LOAD + u // MOE_LOAD + 1)
                pe.wait_ge(s_w_here, 2 * t + 2)
                after(pe, s_act_h, t - 1)
                x = rowsT[:, u // MOE_LOAD, u % MOE_LOAD * P:(u % MOE_LOAD + 1) * P]
                for n in range(2):
                    for f in range(FCHUNKS):
                        here = slice(f * P, (f + 1) * P)
                        mm = pe.matmul(bank_h[:, u % 2, n, here], w_here[:, u % 2, n, here], x, start=True, stop=True)
                mm.then_inc(s_h, 1)

            def results(t, u):
                e = pe.value_load(expert_i[0:1, bass.ds(t, 1)], min_val=0, max_val=EXPERTS - 1)
                pe.wait_ge(s_act_h, t + 1)
                after(pe, s_rows_out, t - 1)
                for f in range(FCHUNKS):
                    mm = pe.matmul(bank_y[:, u % 2, 0:P], act_h[:, u % 4, f * P:(f + 1) * P],
                                   w_2[:, bass.ds(e * FF + f * P, P)], start=(f == 0), stop=(f == FCHUNKS - 1))
                mm.then_inc(s_y_tile, 1)

            pe.wait_ge(s_w_moe, 16 * 3)
            pe.wait_ge(s_expert, 1)
            pe.wait_ge(s_route, ROUTE_TAKEN)

            def experts(i, last=False):
                for u in range(MOE_BODY):
                    t = i * MOE_BODY + u
                    hidden(t, u)
                    if u == MOE_LOAD // 2:
                        turn_rows(i, 1)
                    if u == MOE_LOAD + MOE_LOAD // 2 and not last:
                        turn_rows(i + 1, 0)
                    if u >= 2 or not first(i):
                        results(t - 2, (u - 2) % MOE_BODY)

            turn_rows(0, 0)
            experts(0)
            with pe.Fori(1, ROW_TILES // MOE_BODY - 1) as i:
                experts(i)
            experts(ROW_TILES // MOE_BODY - 1, last=True)
            results(ROW_TILES - 2, MOE_BODY - 2)
            results(ROW_TILES - 1, MOE_BODY - 1)

        @block.scalar
        def _(act):
            act.wait_ge(s_weights, WEIGHTS)
            nc.scalar.activation(a_neg[:], a_log[:], ACT.Exp).then_inc(s_alog, 1)
            for t in range(TAPS):
                act.wait_ge(s_wmul, t + 1)
                nc.scalar.activation(w_conv[:, t, :], l0_banks[:, 0, 0:2 * P], ACT.Copy, scale=0.5
                                     ).then_inc(s_wconv, 1)

            def full(ring, use, it):
                act.wait_ge(ring.full_sem(use), ring.full_at(use, it))
                return ring.bank(use)

            def layer0(u, i):
                if u == 0:
                    nc.scalar.copy(xT[:, TAPS - 1:TAPS - 1 + T], full(l0, "xT", i)).then_inc(l0.free_sem("xT"), 1)
                if u == 1:
                    for h in range(HALVES):
                        if h == 0:
                            after(act, s_du, at(i, 1, 0))
                            after(act, s_y, at(i, HALVES, 0))
                        nc.scalar.activation(xc[:, h, :], full(l0, f"u{h}", i), ACT.Identity,
                                             bias=b_conv[:, h:h + 1]).then_inc(l0.free_sem(f"u{h}"), 1)
                        drained(act, l0, i, f"u{h}")
                        nc.scalar.activation(th[:, h, :], xc[:, h, :], ACT.Tanh).then_inc(s_tanh, 1)
                if u == 2:
                    for h in range(HALVES):
                        bank = full(l0, f"z{h}", i)
                        after(act, s_scan, at(i, 2 * STATES, 0))
                        nc.scalar.activation(push[:, h, :], bank, ACT.Tanh, scale=0.5).then_inc(s_tanh, 1)
                if u == 3:
                    nc.scalar.copy(dt_raw[DT_ROW:DT_ROW + 8, :], full(l0, "xdbl", i)[DT_ROW:DT_ROW + 8, :]
                                   ).then_inc(s_dt_raw, 1)
                if u == 4:
                    for h in range(HALVES):
                        nc.scalar.activation(delta[:, h, :], full(l0, f"dt{h}", i), ACT.Identity,
                                             bias=b_dt[:, h:h + 1]).then_inc(l0.free_sem(f"dt{h}"), 1)
                    drained(act, l0, i, "dt0", "dt1")
                    act.wait_ge(s_xc, at(i, HALVES, HALVES))
                    nc.scalar.activation(th[:], delta[:], ACT.Abs).then_inc(s_sp, 1)
                    act.wait_ge(s_sp, at(i, 3, 1))
                    nc.scalar.activation(th[:], th[:], ACT.Exp, scale=-1.0).then_inc(s_sp, 1)
                if 5 <= u < 5 + STATES:
                    n = u - 5
                    if n == 0:
                        act.wait_ge(s_delta, at(i, HALVES, HALVES))
                    after(act, s_scan, at(i, 2 * STATES, 2 * (n - 1)))
                    for h in range(HALVES):
                        nc.scalar.activation(decay[:, n % 2, h, :], delta[:, h, :], ACT.Exp,
                                             scale=a_neg[:, h, n:n + 1]).then_inc(s_decay, 1)
                if u == 15:
                    nc.scalar.copy(x1T[:], full(l0, "x1T", i)).then_inc(l0.free_sem("x1T"), 1)

            def opening(j):
                nc.scalar.copy(x2T[:], full(l1, "x2T", j)).then_inc(l1.free_sem("x2T"), 1)

            def log_decay(j):
                nc.scalar.activation(sp_in[:], full(l1, "wd", j)[0:ROWS, :], ACT.Identity, bias=b_d[:]
                                     ).then_inc(l1.free_sem("wd"), 1)
                drained(act, l1, j, "wd")
                nc.scalar.activation(sp_ln[:], sp_in[:], ACT.Abs).then_inc(s_dsp, 1)
                act.wait_ge(s_dsp, at(j, 3, 1))
                nc.scalar.activation(sp_ln[:], sp_ln[:], ACT.Exp, scale=-1.0).then_inc(s_dsp, 1)

            def logs(i, j):
                if i is not None:
                    act.wait_ge(s_sp, at(i, 3, 2))
                    nc.scalar.activation(th[:], th[:], ACT.Ln, bias=1.0).then_inc(s_sp, 1)
                if j is not None:
                    act.wait_ge(s_dsp, at(j, 3, 2))
                    nc.scalar.activation(sp_ln[:], sp_ln[:], ACT.Ln, bias=1.0).then_inc(s_dsp, 1)

            def drain(dst, use, j, func=ACT.Copy, scale=1.0):
                nc.scalar.activation(dst, full(l1, use, j), func, scale=scale).then_inc(l1.free_sem(use), 1)

            def project(u, j):
                if u == 0 and first(j):
                    act.wait_ge(s_cleared, 16 * (ROW_TILES // ZERO_ROWS))
                if u not in Q_BY_DVE:
                    drain(q[:, u, :], f"q{u}", j)
                if u >= 2:
                    drained(act, lk, j, f"k{u - 2}")
                drain(tg[:, u % 2, :], f"g{u}", j, ACT.Tanh, 0.5)
                if u == 6:
                    nc.scalar.copy(fall_tok[:].rearrange("p (c h) -> p c h", h=HEADS),
                                   full(l1, "cpT", j)[:, 0:TILES * ROWS].rearrange("p (c r) -> p c r", r=ROWS)[:, :, 0:HEADS]
                                   ).then_inc(l1.free_sem("cpT"), 1)
                if u == 7:
                    nc.scalar.activation(to_end[:], full(l1, "cpd", j)[:, 0:TILES * HEADS].rearrange(
                        "p (c h) -> p c h", h=HEADS), ACT.Exp).then_inc(l1.free_sem("cpd"), 1)

            def decay_mask(g, c, j):
                if g >= 2 or c:
                    drained(act, l1, j, f"S{(g + 2) % 4}_{c if g >= 2 else c - 1}")
                nc.scalar.activation(E[:, g % 2, :], full(l1, f"D{g}_{c}", j), ACT.Exp).then_inc(l1.free_sem(f"D{g}_{c}"), 1)

            def squares(f, c, j):
                act.wait_ge(s_O, at(j, 4 * TILES, 4 * c + 2 * f + 2))
                after(act, s_osq, at(j, 2 * TILES, 2 * c + f))
                nc.scalar.activation(sq[:], o_banks[:, f, :], ACT.Square, accum_out=ssq[:, c, f:f + 1]
                                     ).then_inc(s_osq, 1)

            def turned_out(c, j):
                for f in range(2):
                    nc.scalar.activation(oT[:, 4 * f:4 * f + 4, :],
                                         full(l1, f"OT{f}_{c}", j).rearrange("p (t n) -> p t n", n=P), ACT.Copy
                                         ).then_inc(l1.free_sem(f"OT{f}_{c}"), 1)

            def half_chunk(u, j):
                c, f = divmod(u - PAIRS, 2)
                if f == 0:
                    for n in range(2):
                        drain(v[:, n * T:(n + 1) * T], f"v{n}_{c}", j)
                    after(act, s_og, at(j, 2 * TILES, 2 * c))
                    for n in range(2):
                        drain(tog[:, n * T:(n + 1) * T], f"o{n}_{c}", j, ACT.Tanh, 0.5)
                    after(act, s_qd, at(j, TILES, c))
                    after(act, s_decst, at(j, 2 * (TILES - 2), 2 * max(c - 1, 0)))
                    for n in range(2):
                        nc.scalar.activation(from_start[:, 4 * n:4 * n + 4, :],
                                             full(l1, f"e{n}_{c}", j).rearrange("p (t n) -> p t n", n=P), ACT.Exp
                                             ).then_inc(l1.free_sem(f"e{n}_{c}"), 1)
                    decay_mask(0, c, j)
                    if c:
                        turned_out(c - 1, j)
                    decay_mask(1, c, j)
                else:
                    decay_mask(2, c, j)
                    squares(0, c, j)
                    decay_mask(3, c, j)
                    squares(1, c, j)

            def closing(u, j, it):
                if u == -1:
                    turned_out(TILES - 1, it)
                if u == 4:
                    drain(x3T[:], "x3T", it)
                if u == 5:
                    nc.scalar.copy(logits[:, bass.ds(j * TILES, TILES), :],
                                   full(l1, "route", it)[:, 0:TILES * EXPERTS].rearrange("p (t e) -> p t e", e=EXPERTS)
                                   ).then_inc(l1.free_sem("route"), 1)

            def body(i, j):
                if j is not None:
                    opening(j)
                if i is not None:
                    layer0(0, i)
                if j is not None and not first(j):
                    closing(-1, j - 1, j)
                if j is not None:
                    log_decay(j)
                if i is not None:
                    layer0(1, i)
                for u in range(UNITS):
                    within = state_within(u, i, j)
                    if within is not None:
                        layer0(5 + within, i)
                    if j is not None:
                        project(u, j) if u < PAIRS else half_chunk(u, j)
                        if u < PAIRS and not first(j):
                            closing(u, j - 1, j)
                    for n in L0_STEPS[u] if i is not None else ():
                        if within is None or n != 5 + within:
                            layer0(n, i)
                    if u == LOGS:
                        logs(i, j)

            rounds(act, body)
            for u in range(-1, PAIRS):
                closing(u, B - 1, END)

            act.wait_ge(s_route, ROUTE_BEST)
            nc.scalar.activation(share[:, 1, :], share[:, 0, :], ACT.Exp).then_inc(s_share, 1)

            def turned_rows(i, n):
                g = 2 * i + n
                act.wait_ge(s_turned, g + 1)
                after(act, s_h, MOE_LOAD * (g - 1) if not first(i) else 0)
                nc.scalar.copy(rowsT[:, n, :], bank_rows[:, n, :]).then_inc(s_rowsT, 1)

            def tanh_hidden(t, u):
                act.wait_ge(s_h, t + 1)
                after(act, s_silu, t - 1)
                nc.scalar.activation(tanh_h[:, u % 2, :], bank_h[:, u % 2, 0, :], ACT.Tanh, scale=0.5
                                     ).then_inc(s_tanh_h, 1)

            def result_out(t, u):
                act.wait_ge(s_y_tile, t + 1)
                if u % MOE_LOAD == 0 and not first_pass(t, u):
                    act.wait_ge(s_results[u // MOE_LOAD], stored_before(t, u))
                nc.scalar.copy(rows_out[:, u // MOE_LOAD, u % MOE_LOAD, :], bank_y[:, u % 2, 0:P]).then_inc(s_rows_out, 1)

            def first_pass(t, u):
                return isinstance(t, int) and t < MOE_BODY

            def stored_before(t, u):
                return 2 * (t - u)

            def experts(i, last=False):
                for u in range(MOE_BODY):
                    t = i * MOE_BODY + u
                    tanh_hidden(t, u)
                    if u == MOE_LOAD // 2:
                        turned_rows(i, 1)
                    if u == MOE_LOAD + MOE_LOAD // 2 and not last:
                        turned_rows(i + 1, 0)
                    if u >= 2 or not first(i):
                        result_out(t - 2, (u - 2) % MOE_BODY)

            turned_rows(0, 0)
            experts(0)
            with act.Fori(1, ROW_TILES // MOE_BODY - 1) as i:
                experts(i)
            experts(ROW_TILES // MOE_BODY - 1, last=True)
            result_out(ROW_TILES - 2, MOE_BODY - 2)
            result_out(ROW_TILES - 1, MOE_BODY - 1)

        @block.vector
        def _(dve):
            nc.vector.memset(xT[:, 0:TAPS - 1], 0.0).then_inc(s_prep, 1)
            nc.vector.memset(ones[:], 1.0).then_inc(s_prep, 1)
            nc.vector.memset(state[:], 0.0).then_inc(s_prep, 1)
            nc.vector.memset(zeros, 0.0).then_inc(s_zero, 1)
            dve.wait_ge(s_weights, WEIGHTS)
            for t in range(TAPS):
                if t >= 1:
                    dve.wait_ge(s_wmul, t)
                for c in range(HALVES):
                    nc.vector.tensor_scalar(w_tap[:, c, :], w_inT[:, c, :], taps[:, c, t:t + 1], None,
                                            ALU.mult).then_inc(s_wtap, 1)
            for w in (b_conv, w_out, w_k):
                nc.vector.tensor_scalar(w[:], w[:], 0.5, None, ALU.mult).then_inc(s_prep, 1)
            for t in range(PAIRS):
                nc.vector.tensor_scalar(w_o[:, t, :], w_o[:, t, :], norm_w[:, t:t + 1], 0.5 * HID ** 0.5, ALU.mult, ALU.mult
                                        ).then_inc(s_prep, 1)
            nc.vector.tensor_scalar(w_less[:], w_ffn[:], 0.0, None, ALU.is_lt).then_inc(s_sign, 1)
            nc.vector.tensor_scalar(w_sign[:], w_ffn[:], 0.0, None, ALU.is_gt).then_inc(s_sign, 1)
            dve.wait_ge(s_sign, 2)
            nc.vector.tensor_tensor(w_sign[:], w_sign[:], w_less[:], ALU.subtract).then_inc(s_prep, 1)
            dve.wait_ge(s_alog, 1)
            nc.vector.tensor_scalar(a_neg[:], a_neg[:], -1.0, None, ALU.mult).then_inc(s_prep, 1)
            dve.wait_ge(s_prep, PREPARED)

            def full(ring, use, it):
                dve.wait_ge(ring.full_sem(use), ring.full_at(use, it))
                return ring.bank(use)

            def split(ps, rs, step, base, per, it):
                dve.wait_ge(step, at(it, per, base))
                nc.vector.tensor_copy(ps[PART2:ROWS, :], rs[PART2:ROWS, :]).then_inc(step, 1)
                dve.wait_ge(step, at(it, per, base + 1))
                nc.vector.tensor_tensor(rs[PART3:ROWS, :], rs[PART3:ROWS, :], ps[PART3:ROWS, :], ALU.subtract
                                        ).then_inc(step, 1)
                dve.wait_ge(step, at(it, per, base + 2))
                nc.vector.tensor_copy(ps[PART3:ROWS, :], rs[PART3:ROWS, :]).then_inc(step, 1)

            def deviation(x, step, it):
                for t in range(TILES):
                    nc.vector.bn_stats(stats[:, t, :], x[:, t, :]).then_inc(step, 1)
                dve.wait_ge(step, at(it, LN_STEPS, 4))
                nc.vector.tensor_tensor(mean[:], stats[:, :, 1], stats[:, :, 4], ALU.add).then_inc(step, 1)
                nc.vector.tensor_tensor(apart[:], stats[:, :, 1], stats[:, :, 4], ALU.subtract).then_inc(step, 1)
                nc.vector.tensor_tensor(var[:], stats[:, :, 2], stats[:, :, 5], ALU.add).then_inc(step, 1)
                dve.wait_ge(step, at(it, LN_STEPS, 6))
                nc.vector.tensor_tensor(apart[:], apart[:], apart[:], ALU.mult).then_inc(step, 1)
                nc.vector.tensor_scalar(mean[:], mean[:], 0.5, None, ALU.mult).then_inc(step, 1)
                dve.wait_ge(step, at(it, LN_STEPS, 8))
                nc.vector.scalar_tensor_tensor(var[:], apart[:], P / 4, var[:], ALU.mult, ALU.add).then_inc(step, 1)
                dve.wait_ge(step, at(it, LN_STEPS, 10))
                nc.vector.tensor_scalar(var[:], var[:], 1 / P, LN_EPS, ALU.mult, ALU.add).then_inc(step, 1)

            def normalize(x, scale, done, it):
                dve.wait_ge(scale, at(it, 1, 1))
                for t in range(TILES):
                    nc.vector.tensor_scalar(x[:, t, :], x[:, t, :], mean[:, t:t + 1], rstd[:, t:t + 1],
                                            ALU.subtract, ALU.mult).then_inc(done, 1)

            def layer_norm(x, step, scale, done, it):
                deviation(x, step, it)
                normalize(x, scale, done, it)

            def state_part(n, part, i):
                if n is None:
                    return
                if part == 0:
                    if n == 0:
                        dve.wait_ge(s_du, at(i, 1, 1))
                        drained(dve, l0, i, "z0", "z1")
                    after(dve, s_scan, at(i, 2 * STATES, 2 * n))
                    both = full(l0, f"B{n}", i).unsqueeze(1).broadcast_to([P, HALVES, T])
                    nc.vector.tensor_tensor(push[:], du[:], both, ALU.mult).then_inc(l0.free_sem(f"B{n}"), 1)
                if part in (1, 2):
                    h = part - 1
                    if h == 0:
                        drained(dve, l0, i, f"B{n}")
                        if n:
                            drained(dve, l0, i, f"C{n - 1}")
                    dve.wait_ge(s_decay, at(i, 2 * STATES, 2 * n + h + 1))
                    nc.vector.tensor_tensor_scan(hs[:, h, :], decay[:, n % 2, h, :], push[:, h, :], 0.0,
                                                 ALU.mult, ALU.add).then_inc(s_scan, 1)
                if part == 3:
                    both = full(l0, f"C{n}", i).unsqueeze(1).broadcast_to([P, HALVES, T])
                    dve.wait_ge(s_scan, at(i, 2 * STATES, 2 * n + 2))
                    after(dve, s_ysum, at(i, STATES - 1, 0 if n < 2 else max(n - 2, 1)))
                    nc.vector.tensor_tensor(ch[:, n % 2, :, :], hs[:], both, ALU.mult).then_inc(l0.free_sem(f"C{n}"), 1)

            def layer0(u, i):
                if u == 1:
                    for h in range(HALVES):
                        dve.wait_ge(s_tanh, at(i, 4, h + 1))
                        nc.vector.scalar_tensor_tensor(xc[:, h, :], th[:, h, :], 1.0, xc[:, h, :],
                                                       ALU.add, ALU.mult).then_inc(s_xc, 1)
                if u == 2:
                    for h in range(HALVES):
                        dve.wait_ge(s_tanh, at(i, 4, 3 + h))
                        nc.vector.scalar_tensor_tensor(sz[:, h, :], push[:, h, :], 1.0, full(l0, f"z{h}", i),
                                                       ALU.add, ALU.mult).then_inc(l0.free_sem(f"z{h}"), 1)
                if u == 3:
                    bank = full(l0, "xdbl", i)[0:ROWS, :]
                    dve.wait_ge(s_dt_raw, at(i, 1, 1))
                    nc.vector.tensor_copy(parts[:], bank).then_inc(s_split, 1)
                    dve.wait_ge(s_split, at(i, 4, 1))
                    nc.vector.tensor_tensor(rest[:], bank, parts[:], ALU.subtract).then_inc(l0.free_sem("xdbl"), 1)
                    drained(dve, l0, i, "xdbl")
                    split(parts, rest, s_split, 1, 4, i)
                if 5 <= u < 5 + STATES:
                    for part in range(4):
                        state_part(u - 5, part, i)
                if u == 13:
                    dve.wait_ge(s_ysum, at(i, STATES - 1, STATES - 1))
                    for h in range(HALVES):
                        nc.vector.scalar_tensor_tensor(y[:, h, :], xc[:, h, :], d_skip[:, h:h + 1], y[:, h, :],
                                                       ALU.mult, ALU.add).then_inc(s_ygate, 1)
                    for h in range(HALVES):
                        dve.wait_ge(s_ygate, at(i, HALVES, h + 1))
                        nc.vector.tensor_tensor(y[:, h, :], y[:, h, :], sz[:, h, :], ALU.mult).then_inc(s_y, 1)
                if u == 14:
                    dve.wait_ge(s_x_loaded, at(i, 16, 16))
                    nc.vector.tensor_tensor(x1[:], full(l0, "mix", i).rearrange("p (t d) -> p t d", d=P), x_tok[:],
                                            ALU.add).then_inc(l0.free_sem("mix"), 1)
                    drained(dve, l0, i, "mix")
                    layer_norm(x1, s_ln0, s_rstd0, s_x1, i)
                if u == 15:
                    after(dve, s_x2_taken, at(i, 1, 0))
                    nc.vector.tensor_tensor(x2_new[:], full(l0, "ffn", i).rearrange("p (t d) -> p t d", d=P), x1[:],
                                            ALU.add).then_inc(l0.free_sem("ffn"), 1)
                    drained(dve, l0, i, "ffn")
                    layer_norm(x2_new, s_ln1, s_rstd1, s_x2, i)

            def take(j):
                dve.wait_ge(s_x2, at(j, TILES, TILES))
                if not first(j):
                    dve.wait_ge(s_x3_stored, at(j, 16, 0))
                    dve.wait_ge(l1.full_sem("x3T"), l1.full_at("x3T", j))
                nc.vector.tensor_copy(x3[:], x2_new[:]).then_inc(s_x2_taken, 1)

            def step_sizes(i):
                dve.wait_ge(s_sp, at(i, 3, 3))
                for h in range(HALVES):
                    nc.vector.scalar_tensor_tensor(delta[:, h, :], delta[:, h, :], 0.0, th[:, h, :],
                                                   ALU.max, ALU.add).then_inc(s_delta, 1)
                dve.wait_ge(s_delta, at(i, HALVES, HALVES))
                nc.vector.tensor_tensor(du[:], delta[:], xc[:], ALU.mult).then_inc(s_du, 1)

            def log_decay(j):
                dve.wait_ge(s_dsp, at(j, 3, 3))
                nc.vector.scalar_tensor_tensor(sp_in[:], sp_in[:], 0.0, sp_ln[:], ALU.max, ALU.add).then_inc(s_dlog, 1)
                dve.wait_ge(s_dlog, at(j, 1, 1))
                for c in range(TILES):
                    here = slice(c * P, (c + 1) * P)
                    nc.vector.tensor_tensor_scan(fall[:, here], ones[:], sp_in[:, here], 0.0,
                                                 ALU.mult, ALU.add).then_inc(s_fall, 1)
                dve.wait_ge(s_fall, at(j, TILES, TILES))
                nc.vector.tensor_copy(fall_parts[:], fall[:]).then_inc(s_fsplit, 1)
                dve.wait_ge(s_fsplit, at(j, 5, 1))
                nc.vector.tensor_tensor(fall_rest[:], fall[:], fall_parts[:], ALU.subtract).then_inc(s_fsplit, 1)

            def take_query(u, j):
                nc.vector.tensor_copy(q[:, u, :], full(l1, f"q{u}", j)).then_inc(l1.free_sem(f"q{u}"), 1)

            def project(u, j):
                drained(dve, l1, j, f"g{u}")
                nc.vector.scalar_tensor_tensor(k[:, u, :], tg[:, u % 2, :], 1.0, full(lk, f"k{u}", j),
                                               ALU.add, ALU.mult).then_inc(lk.free_sem(f"k{u}"), 1)

            def mask_scores(g, c, j):
                drained(dve, l1, j, f"D{g}_{c}")
                nc.vector.tensor_tensor(S[:, g % 2, :], full(l1, f"S{g}_{c}", j), E[:, g % 2, :], ALU.mult
                                        ).then_inc(l1.free_sem(f"S{g}_{c}"), 1)

            def gate_out(f, c, j):
                dve.wait_ge(s_O, at(j, 4 * TILES, 4 * c + 2 * f + 2))
                drained(dve, l1, j, f"o{f}_{c}")
                dve.wait_ge(s_osq, at(j, 2 * TILES, 2 * c + f + 1))
                nc.vector.scalar_tensor_tensor(o[:, f * T:(f + 1) * T], tog[:, f * T:(f + 1) * T], 1.0,
                                               o_banks[:, f, :], ALU.add, ALU.mult).then_inc(s_og, 1)

            def sum_squares(c, j):
                dve.wait_ge(s_osq, at(j, 2 * TILES, 2 * c + 2))
                nc.vector.tensor_tensor(rms[:, c:c + 1], ssq[:, c, 0:1], ssq[:, c, 1:2], ALU.add).then_inc(s_rms, 1)

            def residual(c, j, it):
                dve.wait_ge(s_rms_pow, at(j, TILES, c + 1))
                if c == 0:
                    dve.wait_ge(s_x2_taken, at(j, 1, 1))
                nc.vector.scalar_tensor_tensor(x3[:, c, :], full(l1, f"wo_{c}", it)[:, 0:P], rms[:, c:c + 1],
                                               x3[:, c, :], ALU.mult, ALU.add).then_inc(l1.free_sem(f"wo_{c}"), 1)

            def half_chunk(u, i, j):
                within = state_within(u, i, j)
                c, f = divmod(u - PAIRS, 2)
                if f == 0:
                    if c == 0:
                        drained(dve, l1, j, "cpd")
                    for n in range(2):
                        heads = slice(8 * n, 8 * n + 8)
                        nc.vector.tensor_tensor(
                            kd[:, heads, :], full(l1, f"kT{n}_{c}", j).rearrange("p (h d) -> p h d", d=DH),
                            to_end[:, c, heads].unsqueeze(2).broadcast_to([P, 8, DH]), ALU.mult
                        ).then_inc(l1.free_sem(f"kT{n}_{c}"), 1)
                        state_part(within, n, i)
                    if c:
                        sum_squares(c - 1, j)
                    mask_scores(0, c, j)
                    state_part(within, 2, i)
                    mask_scores(1, c, j)
                    state_part(within, 3, i)
                    if c:
                        residual(c - 1, j, j)
                else:
                    mask_scores(2, c, j)
                    state_part(within, 0, i)
                    gate_out(0, c, j)
                    state_part(within, 1, i)
                    mask_scores(3, c, j)
                    state_part(within, 2, i)
                    gate_out(1, c, j)
                    state_part(within, 3, i)
                    if c < TILES - 1:
                        new = full(l1, f"U_{c}", j).rearrange("p (h d) -> p h d", d=DH)
                        if c:
                            drained(dve, l1, j, f"U_{c - 1}")
                            dve.wait_ge(s_half_state, at(j, TILES - 1, c))
                            for rows, at_head in diagonal:
                                nc.vector.tensor_tensor(
                                    state[rows, :, at_head], state[rows, :, at_head],
                                    from_start[rows, :, P - 1:P].broadcast_to([DH, PAIRS, DH]), ALU.mult
                                ).then_inc(s_decst, 1)
                            dve.wait_ge(s_decst, at(j, 2 * (TILES - 2), 2 * c))
                        for n, (rows, at_head) in enumerate(diagonal):
                            if c:
                                ins = nc.vector.tensor_tensor(state[rows, :, at_head], state[rows, :, at_head], new[rows],
                                                              ALU.add)
                            else:
                                ins = nc.vector.tensor_copy(state[rows, :, at_head], new[rows])
                            ins.then_inc(l1.free_sem(f"U_{c}") if n else s_half_state, 1)

            diagonal = [(slice(n * DH, (n + 1) * DH), slice(n * DH, (n + 1) * DH)) for n in range(2)]

            def closing(u, j, it):
                if u == -1:
                    drained(dve, l1, j, *(f"wo_{c}" for c in range(TILES - 1)))
                    sum_squares(TILES - 1, j)
                if u == 0:
                    residual(TILES - 1, j, it)
                if u == 1:
                    drained(dve, l1, it, f"wo_{TILES - 1}")
                    deviation(x3, s_ln3, j)
                if u == 2:
                    normalize(x3, s_rstd3, s_x3, j)

            def body(i, j):
                if j is not None and not first(j):
                    closing(-1, j - 1, j)
                if i is not None:
                    layer0(1, i)
                for u in range(UNITS):
                    if j is not None and u in Q_BY_DVE:
                        take_query(u, j)
                    if u == LOGS + 1:
                        if i is not None:
                            step_sizes(i)
                    if j is not None:
                        project(u, j) if u < PAIRS else half_chunk(u, i, j)
                        if u < PAIRS and not first(j):
                            closing(u, j - 1, j)
                        if u == LOGS + 2:
                            log_decay(j)
                        if u == LOGS + 3:
                            split(fall_parts, fall_rest, s_fsplit, 2, 5, j)
                        if u == PAIRS:
                            take(j)
                    for n in L0_STEPS[u] if i is not None else ():
                        if state_within(u, i, j) is None or not 5 <= n < 5 + STATES:
                            layer0(n, i)

            rounds(dve, body)
            for u in range(-1, PAIRS):
                closing(u, B - 1, END)

            attention_over(dve)
            dve.wait_ge(s_x3_stored, 16 * B)
            wide = [P, TOK_TILES, EXPERTS]
            steps = [0]

            def step(ins):
                steps[0] += 1
                ins.then_inc(s_route, 1)
                dve.wait_ge(s_route, steps[0])

            def each(x):
                return x.unsqueeze(2).broadcast_to(wide)

            rev_all = rev[:].unsqueeze(1).broadcast_to(wide)
            source = logits
            for n in range(2):
                step(nc.vector.tensor_reduce(best[:, n, :], source[:], AX.X, ALU.max))
                step(nc.vector.tensor_tensor(hot[:, n], source[:], each(best[:, n, :]), ALU.is_equal))
                step(nc.vector.tensor_tensor(hot[:, n], hot[:, n], rev_all, ALU.mult))
                step(nc.vector.tensor_reduce(place[:, n, :], hot[:, n], AX.X, ALU.max))
                step(nc.vector.tensor_tensor(hot[:, n], rev_all, each(place[:, n, :]), ALU.is_equal))
                if n == 0:
                    step(nc.vector.scalar_tensor_tensor(work[:], hot[:, 0], -3e38, logits[:], ALU.mult, ALU.add))
                    source = work
            step(nc.vector.tensor_tensor(hot_bf[:], hot[:, 0], hot[:, 1], ALU.add))
            assert steps[0] == ROUTE_HOT
            step(nc.vector.tensor_tensor(share[:, 0, :], best[:, 1, :], best[:, 0, :], ALU.subtract))
            assert steps[0] == ROUTE_BEST
            step(nc.vector.memset(ones_r[:], 1.0))
            dve.wait_ge(s_counted, 1)
            count = [P, TOK_TILES * EXPERTS]
            step(nc.vector.tensor_copy(rank[:], l1_banks[:, 0, 0:count[1]].rearrange("p (t e) -> p t e", e=EXPERTS)))
            step(nc.vector.tensor_copy(total[:], l1_banks[:, 1, 0:count[1]].rearrange("p (t e) -> p e t", e=EXPERTS)))
            assert steps[0] == ROUTE_TAKEN
            for e in range(EXPERTS):
                step(nc.vector.tensor_tensor_scan(upto[:, e, :], ones_r[:], total[:, e, :], 0.0, ALU.mult, ALU.add))
            step(nc.vector.tensor_scalar(count_i[:], upto[:, :, TOK_TILES - 1], float(P - 1), None, ALU.add))
            step(nc.vector.tensor_scalar(count_i[:], count_i[:], 7, None, ALU.arith_shift_right))
            step(nc.vector.tensor_copy(tiles_of[:], count_i[:]))
            step(nc.vector.tensor_tensor_scan(ends[:], ones_r[:, 0:EXPERTS], tiles_of[:], 0.0, ALU.mult, ALU.add))
            step(nc.vector.tensor_tensor(base[:], ends[:], tiles_of[:], ALU.subtract))
            step(nc.vector.tensor_scalar(base[:], base[:], float(P), None, ALU.mult))
            step(nc.vector.tensor_tensor(upto[:], upto[:], total[:], ALU.subtract))
            step(nc.vector.tensor_tensor(upto[:], upto[:], base[:].unsqueeze(2).broadcast_to([P, EXPERTS, TOK_TILES]),
                                         ALU.add))
            step(nc.vector.tensor_tensor(rank[:], rank[:], upto[:].rearrange("p e t -> p t e"), ALU.add))
            for n in range(2):
                step(nc.vector.tensor_tensor(work[:], rank[:], hot[:, n], ALU.mult))
                step(nc.vector.tensor_reduce(place[:, n, :], work[:], AX.X, ALU.add))
            nc.vector.tensor_copy(row_of[:], place[:]).then_inc(s_rows_known, 1)
            step(nc.vector.tensor_tensor(past[:], tile_no[:].unsqueeze(2).broadcast_to([1, ROW_TILES, EXPERTS]),
                                         ends[0:1, :].unsqueeze(1).broadcast_to([1, ROW_TILES, EXPERTS]), ALU.is_ge))
            step(nc.vector.tensor_reduce(expert_f[:], past[:], AX.X, ALU.add))
            step(nc.vector.tensor_scalar(expert_f[:], expert_f[:], float(EXPERTS - 1), None, ALU.min))
            nc.vector.tensor_copy(expert_i[:], expert_f[:]).then_inc(s_expert, 1)
            dve.wait_ge(s_share, 1)
            step(nc.vector.tensor_scalar(share[:, 0, :], share[:, 1, :], 2.0, 2.0, ALU.mult, ALU.add))
            step(nc.vector.reciprocal(share[:, 0, :], share[:, 0, :]))
            step(nc.vector.tensor_tensor(share[:, 1, :], share[:, 1, :], share[:, 0, :], ALU.mult))

            def activate(t, u):
                dve.wait_ge(s_tanh_h, t + 1)
                nc.vector.scalar_tensor_tensor(tanh_h[:, u % 2, :], tanh_h[:, u % 2, :], 1.0, bank_h[:, u % 2, 0, :],
                                               ALU.add, ALU.mult).then_inc(s_silu, 1)
                dve.wait_ge(s_silu, t + 1)
                after(dve, s_y_tile, t - 3)
                nc.vector.tensor_tensor(act_h[:, u % 4, :], tanh_h[:, u % 2, :], bank_h[:, u % 2, 1, :], ALU.mult
                                        ).then_inc(s_act_h, 1)

            def weights_here(t, u):
                e = dve.value_load(expert_i[0:1, bass.ds(t, 1)], min_val=0, max_val=EXPERTS - 1)
                after(dve, s_h, t - 1)
                for n, w in enumerate((w_0, w_1)):
                    nc.vector.tensor_copy(w_here[:, u % 2, n, :], w[:, bass.ds(e * FF, FF)]).then_inc(s_w_here, 1)

            def experts(i):
                for u in range(MOE_BODY):
                    t = i * MOE_BODY + u
                    weights_here(t, u)
                    if u >= 1 or not first(i):
                        activate(t - 1, (u - 1) % MOE_BODY)

            dve.wait_ge(s_w_moe, 16 * 3)
            dve.wait_ge(s_expert, 1)
            experts(0)
            with dve.Fori(1, ROW_TILES // MOE_BODY) as i:
                experts(i)
            activate(ROW_TILES - 1, MOE_BODY - 1)

            dve.wait_ge(s_tokens, 16 * B)
            for b in range(B):
                n, turn_no = b % 2, b // 2
                after(dve, s_out[n], 16 * turn_no)
                dve.wait_ge(s_gathered[n], 16 * 2 * TILES * (turn_no + 1))
                for r in range(2):
                    for t in range(TILES):
                        if r:
                            dve.wait_ge(s_mixed, 2 * TILES * b + t + 1)
                        nc.vector.scalar_tensor_tensor(
                            final[:, n, t, :], gathered[:, n, t, r, :], share[:, r, b * TILES + t:b * TILES + t + 1],
                            final[:, n, t, :] if r else tokens[:, b * TILES + t, :], ALU.mult, ALU.add
                        ).then_inc(s_mixed, 1)
                dve.wait_ge(s_mixed, 2 * TILES * (b + 1))
                layer_norm(final[:, n], s_ln4, s_rstd4, s_final, b)

        @block.gpsimd
        def _(pool):
            nc.gpsimd.memset(minus_half[:], -0.5).then_inc(s_prep, 1)
            nc.gpsimd.memset(rms_eps[:], HID * RMS_EPS).then_inc(s_prep, 1)
            pool.wait_ge(s_prep, PREPARED)

            def layer0(u, i):
                if 5 <= u < 5 + STATES:
                    n = u - 5
                    if n:
                        pool.wait_ge(l0.free_sem(f"C{n}"), l0.full_at(f"C{n}", i))
                    if n == 1 and not first(i):
                        pool.wait_ge(l0.full_sem("mix"), l0.full_at("mix", i - 1))
                    if n == 1:
                        nc.gpsimd.tensor_tensor(y[:], ch[:, 0, :, :], ch[:, 1, :, :], ALU.add).then_inc(s_ysum, 1)
                    if n > 1:
                        pool.wait_ge(s_ysum, at(i, STATES - 1, n - 1))
                        nc.gpsimd.tensor_tensor(y[:], y[:], ch[:, n % 2, :, :], ALU.add).then_inc(s_ysum, 1)
                if u == 14:
                    scale_of(s_ln0, s_rstd0, i)
                if u == 15:
                    scale_of(s_ln1, s_rstd1, i)

            def scale_of(step, scale, it):
                pool.wait_ge(step, at(it, LN_STEPS, LN_STEPS))
                nc.gpsimd.tensor_tensor(rstd[:], var[:], minus_half[:], ALU.pow).then_inc(scale, 1)

            def rms_of(c, j):
                pool.wait_ge(s_rms, at(j, TILES, c + 1))
                nc.gpsimd.tensor_tensor(rms[:, c:c + 1], rms[:, c:c + 1], rms_eps[:], ALU.add
                                        ).then_inc(s_rms_eps, 1)
                pool.wait_ge(s_rms_eps, at(j, TILES, c + 1))
                nc.gpsimd.tensor_tensor(rms[:, c:c + 1], rms[:, c:c + 1], minus_half[:, 0:1], ALU.pow
                                        ).then_inc(s_rms_pow, 1)

            def closing(u, j):
                if u == -1:
                    rms_of(TILES - 1, j)
                if u == 1:
                    scale_of(s_ln3, s_rstd3, j)

            def half_chunk(u, j):
                c, f = divmod(u - PAIRS, 2)
                if f == 0:
                    drained(pool, l1, j, f"e0_{c}", f"e1_{c}", *(f"q{p}" for p in range(PAIRS) if c == 0))
                    after(pool, s_O, at(j, 4 * TILES, 4 * c))
                    nc.gpsimd.tensor_tensor(qd[:], q[:, :, c * P:(c + 1) * P], from_start[:], ALU.mult
                                            ).then_inc(s_qd, 1)
                    if c:
                        rms_of(c - 1, j)

            def body(i, j):
                if j is not None and not first(j):
                    closing(-1, j - 1)
                for u in range(UNITS):
                    if j is not None and u >= PAIRS:
                        half_chunk(u, j)
                    if j is not None and not first(j) and u < PAIRS:
                        closing(u, j - 1)
                    for n in L0_STEPS[u] if i is not None else ():
                        layer0(n, i)

            rounds(pool, body)
            for u in range(-1, PAIRS):
                closing(u, B - 1)

            pool.wait_ge(s_rows_known, 1)
            pool.wait_ge(s_tokens, 16 * B)
            for t in range(TOK_TILES):
                for n in range(2):
                    nc.gpsimd.indirect_dma_start(
                        out=rows_dram, out_offset=bass.IndirectOffsetOnAxis(ap=row_of[:, n, t:t + 1], axis=0),
                        in_=tokens[:, t, :], in_offset=None).then_inc(s_scattered, 16)
            for n in range(2):
                pool.wait_ge(s_results[n], 16 * (ROW_TILES // MOE_BODY))
            for b in range(B):
                n, turn_no = b % 2, b // 2
                if b >= 2:
                    pool.wait_ge(s_mixed, 2 * TILES * (b - 1))
                for t in range(TILES):
                    for r in range(2):
                        nc.gpsimd.indirect_dma_start(
                            out=gathered[:, n, t, r, :], out_offset=None, in_=results_dram,
                            in_offset=bass.IndirectOffsetOnAxis(ap=row_of[:, r, b * TILES + t:b * TILES + t + 1], axis=0)
                        ).then_inc(s_gathered[n], 16)
                if b:
                    scale_of(s_ln4, s_rstd4, b - 1)
            scale_of(s_ln4, s_rstd4, B - 1)


def kernel(**inputs):
    import ml_dtypes
    import concourse.bacc as bacc
    from concourse.bass_utils import run_bass_kernel_spmd

    g = {n: np.ascontiguousarray(v) for n, v in inputs.items()}
    c = shape_constants()
    bf = ml_dtypes.bfloat16

    def rows(w):
        return w.reshape(-1, P, w.shape[1]).transpose(1, 0, 2)

    def thrice(w):
        full = np.zeros((w.shape[0], ROWS), w.dtype)
        for at_col in (0, PART2, PART3):
            full[:, at_col:at_col + w.shape[1]] = w
        return full

    w_in = g["L0_attn_W_in"]
    w_x = thrice(g["L0_attn_W_x"][:, STATES:])
    w_x[:, DT_ROW:DT_ROW + STATES] = g["L0_attn_W_x"][:, :STATES]
    arrays = {
        "x": g["L0_attn_x"],
        "eye": c["eye"], "from_last": c["from_last"], "eye_bf": c["eye"].astype(bf),
        "sel": c["sel"].astype(bf), "nsel": c["nsel"].astype(bf), "nselpair": c["nselpair"].astype(bf),
        "future": c["future"].astype(bf),
        "w_inT": rows(w_in[:, :2 * P].T), "taps": rows(g["L0_attn_dw_kernel"].T), "pw": rows(g["L0_attn_pw_kernel"]),
        "w_z": w_in[:, 2 * P:], "w_x": rows(w_x), "w_dt": g["L0_attn_W_dt"],
        "b_conv": g["L0_attn_conv_bias"].reshape(HALVES, P).T, "b_dt": g["L0_attn_b_dt"].reshape(HALVES, P).T,
        "d_skip": g["L0_attn_D"].reshape(HALVES, P).T, "a_log": rows(g["L0_attn_A_log"]),
        "w_out": rows(g["L0_attn_W_out"]), "w_ffn": g["L0_ffn_weight"].T,
        "w_q": g["L1_attn_Wq"].T, "w_k": g["L1_attn_Wk"].T, "w_v": g["L1_attn_Wv"].T,
        "w_g": g["L1_attn_Wg"].T, "w_og": g["L1_attn_Wog"].T, "w_o": rows(g["L1_attn_Wo"].T),
        "norm_w": g["L1_attn_norm_w"].reshape(PAIRS, P).T, "w_d": thrice(g["L1_attn_Wd"].T),
        "earlier": c["earlier"].astype(bf), "ones_bf": np.ones((P, P), bf), "rev": c["rev"],
        "tile_no": np.arange(moe_tiles(g["L0_attn_x"].shape[0] * T), dtype=np.float32)[None, :],
        "w_0": g["L1_ffn_w0"].transpose(1, 0, 2).reshape(P, EXPERTS * FF),
        "w_1": g["L1_ffn_w1"].transpose(1, 0, 2).reshape(P, EXPERTS * FF),
        "w_2": g["L1_ffn_wo"].reshape(EXPERTS, FCHUNKS, P, P).transpose(2, 0, 1, 3).reshape(P, EXPERTS * FF),
        "b_d": thrice(g["L1_attn_bd"][None, :]).T, "w_route": g["L1_ffn_gate_kernel"],
    }
    arrays = {n: np.ascontiguousarray(v) for n, v in arrays.items()}
    nc = bacc.Bacc("TRN2", target_bir_lowering=False, num_devices=1)
    aps = {n: nc.dram_tensor(n + "_dram", v.shape, mybir.dt.from_np(v.dtype), kind="ExternalInput").ap()
           for n, v in arrays.items()}
    out = nc.dram_tensor("out_dram", g["L0_attn_x"].shape, F32, kind="ExternalOutput").ap()
    build(nc, aps, out)
    r = run_bass_kernel_spmd(nc, [{n + "_dram": v for n, v in arrays.items()}], core_ids=[0])
    return r.results[0]["out_dram"]
```
